# Optimizing a Trainium2 kernel written in Bass

```python
import numpy as np
import jax
import jax.numpy as jnp

def _softmax(x, axis=-1):
    return jax.nn.softmax(x, axis=axis)

def _gelu(x):
    return jax.nn.gelu(x, approximate=True)

def _silu(x):
    return jax.nn.silu(x)

def _sigmoid(x):
    return jax.nn.sigmoid(x)

def _layernorm(x, axis=-1, eps=1e-05):
    m = jnp.mean(x, axis=axis, keepdims=True)
    v = jnp.var(x, axis=axis, keepdims=True)
    return (x - m) / jnp.sqrt(v + eps)

def _scatter_add(tgt, idx, src, axis=0):
    return tgt.at[idx].add(src)

def _segment_sum(src, seg, n):
    return jax.ops.segment_sum(src, seg, n)
kernel_name = 'mk_flamingo_gated_d1_seqx_r8_fb990f'

def setup_inputs(seed: int=0):
    np.random.seed(seed)
    _w = jnp.asarray

    def _rec_inputs():
        import jax
        import jax.numpy as jnp
        _rk = jax.random.key(seed)
        x = 7.22e-05 + 1 * jax.random.normal(jax.random.fold_in(_rk, 1), (32, 64, 256), jnp.float32)
        _lenS = 64 - jax.random.randint(jax.random.fold_in(_rk, 7), (32,), 0, max(1, 64 // 4) + 1, jnp.int32)
        _lenS2 = 64 - jax.random.randint(jax.random.fold_in(_rk, 8), (32,), 0, max(1, 64 // 4) + 1, jnp.int32)
        _ctx_2048P = jax.random.normal(jax.random.fold_in(_rk, 11), (32, 16, 256), jnp.float32)
        _ctx_2048c = jax.random.dirichlet(jax.random.fold_in(_rk, 511), 0.3 * jnp.ones((16,), jnp.float32), (32, 64))
        _ctx_2048t = jnp.einsum('bsk,bkd->bsd', _ctx_2048c, _ctx_2048P)
        _ctx_2048t = _ctx_2048t * jax.lax.rsqrt(jnp.mean(jnp.square(_ctx_2048t)) + 1e-12) * 0.953939
        ctx_2048 = 4.13588e-05 + 0.999923 * (_ctx_2048t + 0.3 * jax.random.normal(jax.random.fold_in(_rk, 611), (32, 64, 256), jnp.float32))
        _g = jax.random.normal(jax.random.fold_in(_rk, 9001), (2, 1), jnp.float32)
        _g = jnp.sign(_g) * jnp.maximum(jnp.abs(_g), 1.0) + (_g == 0) * 1.0
        g_xattn = _g[0]
        g_ffn = _g[1]
        return (x, ctx_2048, g_xattn, g_ffn)
    x, ctx_2048, g_xattn, g_ffn = _rec_inputs()

    def _L0_xattn_setup():
        import jax, jax.numpy as jnp
        import numpy as np
        N_HEAD = 8
        key = jax.random.key(seed)
        k1, k2, k3 = jax.random.split(key, 3)
        B, D, L = (4, 128, 256)
        q = jax.random.normal(k1, (B, D, L), dtype=jnp.float32)
        k = jax.random.normal(k2, (B, D, L), dtype=jnp.float32)
        v = jax.random.normal(k3, (B, D, L), dtype=jnp.float32)
        gamma = jnp.ones((), dtype=jnp.float32)
        return {'q': q, 'k': k, 'v': v, 'gamma': gamma}
    _L0_xattn_all = _L0_xattn_setup()
    _L0_xattn_in = {k: v for k, v in _L0_xattn_all.items() if k in ('gamma',)}
    del _L0_xattn_all

    def _L0_ffn_setup():
        import jax, jax.numpy as jnp
        import numpy as np
        ALPHA = 1.702
        LIMIT = 7.0
        TOP_K = 4
        B, S, H = (1, 128, 256)
        E, D = (16, 256)
        key = jax.random.key(seed)
        ks = jax.random.split(key, 7)
        s = 0.02
        return {'hidden_states': jax.random.normal(ks[0], (B, S, H), dtype=jnp.float32), 'router_weight': jax.random.normal(ks[1], (E, H), dtype=jnp.float32) * s, 'router_bias': jax.random.normal(ks[2], (E,), dtype=jnp.float32) * s, 'gate_up_proj': jax.random.normal(ks[3], (E, H, 2 * D), dtype=jnp.float32) * s, 'gate_up_proj_bias': jax.random.normal(ks[4], (E, 2 * D), dtype=jnp.float32) * s, 'down_proj': jax.random.normal(ks[5], (E, D, H), dtype=jnp.float32) * s, 'down_proj_bias': jax.random.normal(ks[6], (E, H), dtype=jnp.float32) * s}
    _L0_ffn_all = _L0_ffn_setup()
    _L0_ffn_in = {k: v for k, v in _L0_ffn_all.items() if k in ('router_weight', 'router_bias', 'gate_up_proj', 'gate_up_proj_bias', 'down_proj', 'down_proj_bias')}
    del _L0_ffn_all
    return {'x': x, 'ctx_2048': ctx_2048, 'g_xattn': g_xattn, 'g_ffn': g_ffn, 'L0_xattn_gamma': _L0_xattn_in['gamma'], 'L0_ffn_router_weight': _L0_ffn_in['router_weight'], 'L0_ffn_router_bias': _L0_ffn_in['router_bias'], 'L0_ffn_gate_up_proj': _L0_ffn_in['gate_up_proj'], 'L0_ffn_gate_up_proj_bias': _L0_ffn_in['gate_up_proj_bias'], 'L0_ffn_down_proj': _L0_ffn_in['down_proj'], 'L0_ffn_down_proj_bias': _L0_ffn_in['down_proj_bias']}

def reference(x, ctx_2048, g_xattn, g_ffn, L0_xattn_gamma, L0_ffn_router_weight, L0_ffn_router_bias, L0_ffn_gate_up_proj, L0_ffn_gate_up_proj_bias, L0_ffn_down_proj, L0_ffn_down_proj_bias):
    import jax
    import jax.numpy as jnp

    def _L0_xattn_ref(q, k, v, gamma):
        import jax, jax.numpy as jnp
        import numpy as np
        N_HEAD = 8
        B, Dq, Lq = q.shape
        Dv, Lk = (v.shape[-2], v.shape[-1])
        h = N_HEAD
        dq = Dq // h
        dv = Dv // h
        qh = q.reshape(B, h, dq, Lq)
        kh = k.reshape(B, h, dq, Lk)
        vh = v.reshape(B, h, dv, Lk)
        scale = 1.0 / jnp.sqrt(jnp.asarray(dq, dtype=q.dtype))
        qk = jnp.einsum('bhdq,bhdl->bhql', qh, kh) * scale
        sm = jax.nn.softmax(qk, axis=-1)
        ret = jnp.einsum('bhql,bhdl->bhdq', sm, vh)
        ret = ret.reshape(B, Dv, Lq)
        return gamma * ret

    def _L0_ffn_ref(hidden_states, router_weight, router_bias, gate_up_proj, gate_up_proj_bias, down_proj, down_proj_bias):
        import jax, jax.numpy as jnp
        import numpy as np
        ALPHA = 1.702
        LIMIT = 7.0
        TOP_K = 4
        B, S, H = (1, 128, 256)
        E, D = (16, 256)
        batch, seq, hdim = hidden_states.shape
        x = hidden_states.reshape(-1, hdim)
        T = x.shape[0]
        logits = x @ router_weight.T + router_bias
        top_val, top_idx = jax.lax.top_k(logits, TOP_K)
        top_val = jax.nn.softmax(top_val, axis=-1)
        router_scores = jnp.zeros_like(logits).at[jnp.arange(T)[:, None], top_idx].set(top_val)
        gate_up = jnp.einsum('th,ehd->etd', x, gate_up_proj) + gate_up_proj_bias[:, None, :]
        gate = gate_up[..., ::2]
        up = gate_up[..., 1::2]
        gate = jnp.minimum(gate, LIMIT)
        up = jnp.clip(up, -LIMIT, LIMIT)
        glu = gate * jax.nn.sigmoid(gate * ALPHA)
        out = jnp.einsum('etd,edh->eth', (up + 1.0) * glu, down_proj) + down_proj_bias[:, None, :]
        out = out * router_scores.T[:, :, None]
        out = out.sum(axis=0)
        return out.reshape(batch, seq, hdim)
    x = x + jnp.tanh(g_xattn[0]) * _L0_xattn_ref(_layernorm(x, axis=-1), ctx_2048, ctx_2048, L0_xattn_gamma)
    x = x + jnp.tanh(g_ffn[0]) * _L0_ffn_ref(_layernorm(x, axis=-1), L0_ffn_router_weight, L0_ffn_router_bias, L0_ffn_gate_up_proj, L0_ffn_gate_up_proj_bias, L0_ffn_down_proj, L0_ffn_down_proj_bias)
    return x

_drawn_inputs = setup_inputs


def setup_inputs(seed=0):
    import zlib

    import numpy as np

    out = dict(_drawn_inputs(seed))
    spreads = {}
    factors = {'L0_ffn_router_weight': 2.862,
     'L0_ffn_router_bias': 25.836,
     'L0_ffn_gate_up_proj_bias': 34.473,
     'L0_ffn_down_proj_bias': 7.615}
    for name, (base, spread) in spreads.items():
        noise = np.random.default_rng([zlib.crc32(name.encode()), seed]).standard_normal(out[name].shape)
        drawn = base * np.exp(spread * noise) if base else spread * noise
        out[name] = jnp.asarray(drawn.astype(out[name].dtype))
    for name, factor in factors.items():
        out[name] = (out[name] * factor).astype(out[name].dtype)
    return out
```

```python
from contextlib import ExitStack

import concourse.bass as bass
from concourse import mybir

F32 = mybir.dt.float32
BF16 = mybir.dt.bfloat16
U32 = mybir.dt.uint32
I32 = mybir.dt.int32
ALU = mybir.AluOpType
ACT = mybir.ActivationFunctionType
AX = mybir.AxisListType
IndexOnAxis = bass.IndirectOffsetOnAxis

P = 128
EPS = 1e-5
ALPHA = 1.702
LIMIT = 7.0
HEADS = 8
TOPK = 4
MROW = 96
MB_PARTS = 3


def flamingo_gated_kernel(nc, x, ctx_in, g_xattn, g_ffn, gamma, router_w, router_b,
                          gate_up, gate_up_b, down, down_b, out):
    NB, CH, L = x.shape
    DH = CH // HEADS
    E, H, F2 = gate_up.shape
    D = F2 // 2
    TOK = NB * CH
    NT = TOK // P
    PAIRS = 2 * HEADS
    HC = H // P
    SCALE = float(DH) ** -0.5
    STK = 6 * DH
    REGION = TOK + P
    ROWS = E * REGION + P
    PW = H + E
    MT = TOK * TOPK // P + E
    SKIP = 2 * TOK * TOPK
    assert (P, L, MT % 4) == (2 * CH, H, 0)

    x_rows = x.rearrange("b c l -> (b c) l")
    ctx_rows = ctx_in.rearrange("b c l -> (b c) l")
    out_rows = out.rearrange("b c l -> (b c) l")

    q_parts = nc.dram_tensor("q_parts", [NB * HEADS, MB_PARTS * DH, L], BF16, kind="Internal").ap()
    k_parts = nc.dram_tensor("k_parts", [NB * HEADS, MB_PARTS * DH, L], BF16, kind="Internal").ap()
    att_raw = nc.dram_tensor("att_raw", [NB * 2, P, L], F32, kind="Internal").ap()
    rden_dram = nc.dram_tensor("rden_dram", [NB * HEADS, L], F32, kind="Internal").ap()
    xd = nc.dram_tensor("xd", [ROWS, PW], F32, kind="Internal").ap()
    yd = nc.dram_tensor("yd", [TOPK * TOK, H], F32, kind="Internal").ap()

    with ExitStack() as stack:
        def sb(name, shape, dt):
            return stack.enter_context(nc.sbuf_tensor(name, shape, dt))

        def sem(name):
            return stack.enter_context(nc.semaphore(name))

        bank = [stack.enter_context(nc.psum_tensor(f"bank{i}", [P, 512], F32)) for i in range(8)]
        S1, ST = bank[0:2], bank[2:4]
        PV, MVB, HB, RB = bank[4:8]
        GU, XTB, ATB, YB = bank[0:2], bank[2], bank[3], bank[4:6]

        wgu = sb("wgu", [P, E, HC, F2], F32)
        wdn = sb("wdn", [P, E, HC, H], F32)
        xs = sb("xs", [P, NT, L], F32)
        area = sb("area", [P, 3 * 4096], F32)
        cs = area[:, 0:512].rearrange("p (s l) -> p s l", s=2)
        cv = area[:, 512:1024].rearrange("p (s l) -> p s l", s=2)
        qst = area[:, 4096:8192].bitcast(BF16).rearrange("p (s j l) -> p s j l", s=4, j=HEADS)
        kst = area[:, 8192:12288].bitcast(BF16).rearrange("p (s j l) -> p s j l", s=4, j=HEADS)
        bias_gu = area[:, 0:E * F2].rearrange("p (e f) -> p e f", e=E)
        bias_dn = area[:, E * F2:E * F2 + E * H].rearrange("p (e f) -> p e f", e=E)
        work = sb("work", [P, 7680], F32)
        prob = work[:, 0:4096].rearrange("p (s l) -> p s l", s=HEADS)
        vt = work[:, 4096:5120].rearrange("p (s c j v) -> p s c j v", s=2, c=2, j=PAIRS)
        osb = work[:, 5120:5632]
        qf = work[:, 5632:5888]
        kr = work[:, 5888:6144]
        qs = work[:, 6144:6912].bitcast(BF16).rearrange("p (s n l) -> p s n l", s=2, n=MB_PARTS)
        ks = work[:, 6912:7680].bitcast(BF16).rearrange("p (s n l) -> p s n l", s=2, n=MB_PARTS)
        xt = work[:, 0:4 * PW].rearrange("p (s f) -> p s f", s=4)
        o = 4 * PW
        ysb = work[:, o:o + 4 * H].rearrange("p (s f) -> p s f", s=4)
        o += 4 * H
        xT = work[:, o:o + 2 * H].rearrange("p (s f) -> p s f", s=2)
        o += 2 * H
        actT = work[:, o:o + 2 * D].rearrange("p (s f) -> p s f", s=2)
        o += 2 * D
        gub = work[:, o:o + 2 * F2].rearrange("p (s f two) -> p s f two", s=2, two=2)
        o += 2 * F2
        glu = work[:, o:o + 2 * D].rearrange("p (s f) -> p s f", s=2)
        o += 2 * D
        act = work[:, o:o + 2 * D].rearrange("p (s f) -> p s f", s=2)
        assert o + 2 * D <= 7680
        yk = area[:, 0:2 * TOPK * H].rearrange("p (s k f) -> p s k f", s=2, k=TOPK)
        fin = area[:, 2048:2048 + 2 * H].rearrange("p (s f) -> p s f", s=2)

        st1 = sb("st1", [P, 6], F32)
        mv1 = sb("mv1", [P, 2, 2], F32)
        rs1 = sb("rs1", [P, 2, 2], F32)
        st2 = sb("st2", [P, 6], F32)
        mv2 = sb("mv2", [P, 2, 2], F32)
        rs2 = sb("rs2", [P, 2, 2], F32)
        mx = sb("mx", [P, 2, PAIRS], F32)
        mrem = sb("mrem", [P, 2, PAIRS], F32)
        mpart = sb("mpart", [P, 2, MB_PARTS, PAIRS], BF16)
        mT = sb("mT", [MB_PARTS * PAIRS, 2, P], BF16)
        nat = sb("nat", [P, 2, L], F32)
        den = sb("den", [P, 2, 32], F32)
        rden = sb("rden", [P, 2, 32], F32)
        rdb = sb("rdb", [P, L], F32)
        pay = sb("pay", [P, 2, PW], F32)
        hT = sb("hT", [P, HC, P], F32)
        zpay = sb("zpay", [P, PW], F32)
        wr = sb("wr", [P, HC, E], F32)
        wr_nat = sb("wr_nat", [E, H], F32)
        br = sb("br", [P, E], F32)
        lg = sb("lg", [P, E], F32)
        top = sb("top", [P, NT, 8], F32)
        best = sb("best", [P, 8], F32)
        tidx = sb("tidx", [P, 8], U32)
        tidf = sb("tidf", [P, TOPK], F32)
        hot = sb("hot", [P, TOPK, E], F32)
        tmp = sb("tmp", [P, TOPK, E], F32)
        dst = sb("dst", [P, E], F32)
        pick = sb("pick", [P, 2, E], BF16)
        seen = sb("seen", [P, 2, E], BF16)
        slot_base = sb("slot_base", [P, E], F32)
        slots = sb("slots", [P, 2, TOPK], U32)
        wts = sb("wts", [P, NT, TOPK], F32)
        wsum = sb("wsum", [P, NT], F32)
        gates = sb("gates", [P, 3], F32)
        ident = sb("ident", [P, P], F32)
        identb = sb("identb", [P, P], BF16)
        before = sb("before", [P, P], BF16)
        ones = sb("ones", [P, P], BF16)
        minus_half = sb("minus_half", [P, 1], F32)
        iota_i = work[:, 0:3 * TOPK * E].bitcast(I32).rearrange("p (n k e) -> p n k e", n=3, k=TOPK)
        iota_f = sb("iota_f", [P, 3, TOPK, E], F32)
        e_iota, k_base, e_region = iota_f[:, 0], iota_f[:, 1], iota_f[:, 2, 0]
        tok_i = sb("tok_i", [P, NT], I32)
        tok_f = sb("tok_f", [P, NT], F32)
        tile_i = sb("tile_i", [1, MT], I32)
        tile_f = sb("tile_f", [1, MT], F32)
        cnt = sb("cnt", [1, 8, E], F32)
        cnti = sb("cnti", [1, 2, E], I32)
        cmp = work[0:1, 0:MT * E].rearrange("p (i e) -> p i e", e=E)
        cmpn = work[0:1, MT * E:2 * MT * E].rearrange("p (i e) -> p i e", e=E)
        tabf = sb("tabf", [1, 6, MT], F32)
        tab = sb("tab", [1, 2, MT], I32)
        padrow = sb("padrow", [1, E], I32)
        idxc = sb("idxc", [P, 4], U32)

        names = """passed x_in_first x_in_rest small_in w_in bias_in consts gates_ready wr_T wr_ready
            stats1 rstd1 q_ready k1_ready q1_ready rem_ready k2q2_ready split_ready stats1_link rstd1_link
            scores scores_T max_ready exp_ready pv_ready mpart_ready mpart_link m_T m_T_copied
            v_T v_T_copied o_copied rden_ready x1_ready x1_link stats2 stats2_link rstd2 rstd2_link h_ready h_T
            h_T_copied logits route_link route1 ranks route2 scattered counts table_link table_ready pads_in
            x_T x_T_copied gu_ready act_T act_T_copied y_ready y_copied biased gate_ready sig_ready act_link
            act_ready dest_ready wts_link wts_ready exp_w fin_ready rd_out zero_in setup_link sum_link pow_link""".split()
        S = {n: sem(n) for n in names}
        parts_out = [sem(f"parts_out{i}") for i in range(2)]
        stk_in = [sem(f"stk_in{i}") for i in range(4)]
        mrow_in = [sem(f"mrow_in{i}") for i in range(4)]
        cs_in = [sem(f"cs_in{i}") for i in range(2)]
        cv_in = [sem(f"cv_in{i}") for i in range(2)]
        o_out = sem("o_out")
        nat_in = [sem(f"nat_in{i}") for i in range(2)]
        rdb_in = sem("rdb_in")
        sc_out = [sem(f"sc_out{i}") for i in range(2)]
        xt_in = [sem(f"xt_in{i}") for i in range(4)]
        y_out = [sem(f"y_out{i}") for i in range(4)]
        yk_in = [sem(f"yk_in{i}") for i in range(2)]
        fin_out = [sem(f"fin_out{i}") for i in range(2)]

        class Step:
            def __init__(self, half, odd):
                self.half, self.odd, self.loop = half, odd, not isinstance(half, int)

            def on(self, lag):
                return self.loop or 0 <= 2 * self.half + self.odd - lag < NT

            def tile(self, lag):
                a, odd = divmod(self.odd - lag, 2)
                return 2 * self.half + 2 * a + odd, self.half + a, odd

            def least(self, v, small):
                return self.loop or v >= small

        LAST = NT + 6

        def steps(eng, body):
            for t in range(-1, 6):
                body(Step(t // 2, t % 2))
            with eng.Fori(3, 7) as half:
                body(Step(half, 0))
                body(Step(half, 1))
            for t in range(14, LAST):
                body(Step(t // 2, t % 2))

        def wait(eng, step, s, v):
            if step.least(v, 1):
                eng.wait_ge(s, v)

        def settle(eng):
            eng.sem_inc(S["passed"], 1)

        def chain(eng, s, per, u):
            count = [0]

            def link(ins):
                count[0] += 1
                assert count[0] <= per
                ins.then_inc(s, 1)
                eng.wait_ge(s, u * per + count[0])
            return link

        def chunk_loop(eng, body):
            for i in range(-1, 4):
                body(i // 4, i % 4)
            with eng.Fori(1, MT // 4 - 1) as quarter:
                for r in range(4):
                    body(quarter, r)
            for i in range(MT - 4, MT + 2):
                body(i // 4, i % 4)

        def etile(quarter, r, lag):
            a, slot = divmod(r - lag, 4)
            i = 4 * quarter + 4 * a + slot
            return i, quarter + a, slot, (not isinstance(i, int)) or 0 <= i < MT

        block = stack.enter_context(nc.Block())

        @block.sync
        def _(sp):
            xv = x_rows.rearrange("(t p) l -> p t l", p=P)
            sp.dma_start(xs[:, 0], xv[:, 0]).then_inc(S["x_in_first"], 16)
            for t in range(2):
                sp.dma_start(cs[:, t], ctx_rows[P * t:P * (t + 1)]).then_inc(cs_in[t], 16)
            sp.dma_start(xs[:, 1:NT], xv[:, 1:NT]).then_inc(S["x_in_rest"], 16)
            sp.dma_start(gates[:, 0:1], g_xattn.rearrange("(a b) -> a b", a=1).to_broadcast([P, 1])).then_inc(S["small_in"], 16)
            sp.dma_start(gates[:, 1:2], g_ffn.rearrange("(a b) -> a b", a=1).to_broadcast([P, 1])).then_inc(S["small_in"], 16)
            sp.dma_start(gates[:, 2:3], gamma.to_broadcast([P, 1])).then_inc(S["small_in"], 16)
            sp.dma_start(br[:], router_b.rearrange("(a e) -> a e", a=1).to_broadcast([P, E])).then_inc(S["small_in"], 16)
            sp.dma_start(wr_nat[:], router_w).then_inc(S["small_in"], 16)

            def body(s):
                if s.on(3):
                    u, uh, r = s.tile(3)
                    sp.wait_ge(o_out, 32 * (u + 1))
                    settle(sp)
                    src = att_raw[bass.ds(4 * u, 4)].rearrange("a (j r) l -> (a j) r l", r=32)
                    wait(sp, s, S["x1_ready"], u - 1)
                    wait(sp, s, S["rden_ready"], u - 1)
                    sp.dma_start(nat[:, r], src[:, 0:DH, :]).then_inc(nat_in[r], 16)
                    sp.dma_start(den[:, r], src[:, DH, :].rearrange("a (s i) -> a s i", s=8)).then_inc(nat_in[r], 16)
                if s.on(4):
                    u, uh, r = s.tile(4)
                    sp.wait_ge(S["rd_out"], 16 * (u + 1))
                    wait(sp, s, S["x1_ready"], u)
                    src = rden_dram[bass.ds(16 * u, 16)].unsqueeze(1).to_broadcast([16, DH, L])
                    sp.dma_start(rdb[:], src).then_inc(rdb_in, 16)
                if s.on(-1):
                    u, uh, r = s.tile(-1)
                    wait(sp, s, S["v_T"], u - 1)
                    sp.dma_start(cv[:, r], ctx_rows[bass.ds(P * u, P)]).then_inc(cv_in[r], 16)
                if s.on(-2) and (s.loop or 2 * s.half + s.odd >= 0):
                    u, uh, r = s.tile(-2)
                    sp.wait_ge(S["rem_ready"], u - 1)
                    sp.dma_start(cs[:, r], ctx_rows[bass.ds(P * u, P)]).then_inc(cs_in[r], 16)
                if s.on(0):
                    t = s.tile(0)[0]
                    sp.dma_start(wgu[:, t], gate_up[t].rearrange("(c p) f -> p c f", p=P)).then_inc(S["w_in"], 16)
                    sp.dma_start(wdn[:, t], down[t].rearrange("(c p) f -> p c f", p=P)).then_inc(S["w_in"], 16)
                if s.on(-1):
                    u, uh, r = s.tile(-1)
                    sp.wait_ge(S["split_ready"], u + 1)
                    for parts, dram in ((qs, q_parts), (ks, k_parts)):
                        to = dram[bass.ds(PAIRS * u, PAIRS)].rearrange("a (s d) l -> a s d l", s=MB_PARTS)
                        for n in range(MB_PARTS):
                            sp.dma_start(to[:, n], parts[:, r, n]).then_inc(parts_out[r], 16)
                    sp.wait_ge(parts_out[r], 96 * (uh + 1))
                    for b in range(2):
                        slot = 2 * r + b
                        wait(sp, s, S["scores_T"], PAIRS * (u - 2) + HEADS * (b + 1))
                        lo = PAIRS * u + HEADS * b
                        fq = q_parts[bass.ds(lo, HEADS)].rearrange("a r l -> r a l")
                        fk = k_parts[bass.ds(lo, HEADS)].rearrange("a r l -> r a l")
                        for row, part, n in ((0, 0, 1), (DH, 0, 1), (2 * DH, 0, 3), (5 * DH, 1, 1)):
                            sp.dma_start(qst[row:row + n * DH, slot], fq[part * DH:(part + n) * DH]).then_inc(stk_in[slot], 16)
                        for row, part, n in ((0, 1, 2), (2 * DH, 0, 1), (3 * DH, 0, 1), (4 * DH, 0, 2)):
                            sp.dma_start(kst[row:row + n * DH, slot], fk[part * DH:(part + n) * DH]).then_inc(stk_in[slot], 16)
                if s.on(3):
                    u, uh, r = s.tile(3)
                    sp.wait_ge(S["rden_ready"], u + 1)
                    to = rden_dram[bass.ds(16 * u, 16)].rearrange("a (s i) -> (a s) i", s=8)
                    sp.dma_start(to, rden[:, r]).then_inc(S["rd_out"], 16)
                if not s.loop and 2 * s.half + s.odd == NT + 1:
                    sp.wait_ge(S["scores_T"], NT * PAIRS)
                    sp.dma_start(bias_gu, gate_up_b.unsqueeze(0).to_broadcast([P, E, F2])).then_inc(S["bias_in"], 16)
                    sp.dma_start(bias_dn, down_b.unsqueeze(0).to_broadcast([P, E, H])).then_inc(S["bias_in"], 16)

            sp.wait_ge(S["consts"], 1)
            sp.dma_start(xd[E * REGION:ROWS], zpay[:]).then_inc(S["zero_in"], 16)
            steps(sp, body)

            sp.wait_ge(S["table_ready"], 1)
            with sp.Fori(0, E) as e:
                row = sp.value_load(padrow[0:1, bass.ds(e, 1)], min_val=0, max_val=E * REGION - P)
                sp.dma_start(xd[bass.ds(row, P)], zpay[:]).then_inc(S["pads_in"], 16)
            sp.wait_ge(S["pads_in"], 16 * E)
            sp.wait_ge(S["zero_in"], 16)
            for r in range(2):
                sp.wait_ge(sc_out[r], 16 * TOPK * NT // 2)

            def expert_loads(quarter, r):
                i, iq, slot, on = etile(quarter, r, -1)
                if on:
                    if not isinstance(iq, int) or iq >= 1:
                        sp.wait_ge(S["x_T"], i - 3)
                        sp.wait_ge(S["dest_ready"], i - 3)
                    row = sp.value_load(tab[0:1, 0, bass.ds(i, 1)], min_val=0, max_val=ROWS - P)
                    sp.dma_start(xt[:, slot], xd[bass.ds(row, P)]).then_inc(xt_in[slot], 16)
            chunk_loop(sp, expert_loads)

            for r in range(4):
                sp.wait_ge(y_out[r], 16 * (MT // 4))
            yv = yd.rearrange("(k t p) f -> t p k f", k=TOPK, p=P)
            ov = out_rows.rearrange("(t p) l -> t p l", p=P)
            for u in range(NT + 1):
                if u < NT:
                    if u >= 2:
                        sp.wait_ge(S["fin_ready"], u - 1)
                    sp.dma_start(yk[:, u % 2], yv[u]).then_inc(yk_in[u % 2], 16)
                if u >= 1:
                    sp.wait_ge(S["fin_ready"], u)
                    sp.dma_start(ov[u - 1], fin[:, (u - 1) % 2]).then_inc(fin_out[(u - 1) % 2], 16)
            for r in range(2):
                sp.wait_ge(fin_out[r], 16 * (NT // 2))

        @block.gpsimd
        def _(pool):
            link = chain(pool, S["setup_link"], 12, 0)
            link(nc.gpsimd.memset(zpay[:, 0:H], 0.0))
            link(nc.gpsimd.memset(zpay[:, H:PW].bitcast(U32), SKIP))
            link(nc.gpsimd.memset(qst[:], 0.0))
            link(nc.gpsimd.memset(kst[:], -1.0))
            link(nc.gpsimd.memset(ident[:], 0.0))
            link(nc.gpsimd.affine_select(out=ident[:], in_=ident[:], compare_op=ALU.not_equal, fill=1.0, base=0,
                                         pattern=[[-1, P]], channel_multiplier=1))
            link(nc.gpsimd.tensor_copy(identb[:], ident[:]))
            link(nc.gpsimd.memset(ones[:], 1.0))
            link(nc.gpsimd.affine_select(out=before[:], in_=ones[:], compare_op=ALU.is_gt, fill=0.0, base=0,
                                         pattern=[[1, P]], channel_multiplier=-1))
            nc.gpsimd.memset(minus_half[:], -0.5)
            nc.gpsimd.memset(vt[:, :, :, :, DH:2 * DH], 1.0)
            nc.gpsimd.memset(seen[:], 0.0)
            nc.gpsimd.iota(iota_i[:, 0], pattern=[[0, TOPK], [1, E]], base=0, channel_multiplier=0)
            nc.gpsimd.iota(iota_i[:, 1], pattern=[[TOK, TOPK], [0, E]], base=0, channel_multiplier=0)
            nc.gpsimd.iota(iota_i[:, 2], pattern=[[0, TOPK], [REGION, E]], base=0, channel_multiplier=0)
            nc.gpsimd.iota(tile_i[:], pattern=[[1, MT]], base=0, channel_multiplier=0)
            link(nc.gpsimd.iota(tok_i[:], pattern=[[P, NT]], base=0, channel_multiplier=1))
            nc.gpsimd.tensor_copy(iota_f[:], iota_i[:])
            nc.gpsimd.tensor_copy(tile_f[:], tile_i[:])
            link(nc.gpsimd.tensor_copy(tok_f[:], tok_i[:]))
            nc.gpsimd.tensor_copy(tok_f[:], tok_f[:]).then_inc(S["consts"], 1)

            def rstd(mv, rs, u, r, got, link_sem, done):
                pool.wait_ge(got, u + 1)
                settle(pool)
                link = chain(pool, link_sem, 1, u)
                link(nc.gpsimd.tensor_scalar(rs[:, r, 0:1], mv[:, r, 1:2], EPS, None, ALU.add))
                nc.gpsimd.tensor_tensor(rs[:, r, 1:2], rs[:, r, 0:1], minus_half[:], ALU.pow).then_inc(done, 1)

            def max_parts(s, b):
                t = s.tile(0)[0]
                n = 2 * t + b
                pool.wait_ge(S["max_ready"], HEADS * (n + 1))
                link = chain(pool, S["mpart_link"], 3, n)
                wait(pool, s, S["m_T"], n - 1)
                settle(pool)
                link(nc.gpsimd.tensor_copy(mpart[:, b, 0], mx[:, b]))
                link(nc.gpsimd.tensor_tensor(mrem[:, b], mx[:, b], mpart[:, b, 0], ALU.subtract))
                settle(pool)
                link(nc.gpsimd.tensor_copy(mpart[:, b, 1], mrem[:, b]))
                nc.gpsimd.tensor_tensor(mpart[:, b, 2], mrem[:, b], mpart[:, b, 1], ALU.subtract).then_inc(S["mpart_ready"], 1)

            def body(s):
                if s.on(-1):
                    u, uh, r = s.tile(-1)
                    rstd(mv1, rs1, u, r, S["stats1"], S["rstd1_link"], S["rstd1"])
                    pool.wait_ge(S["k1_ready"], u + 1)
                    nc.gpsimd.tensor_tensor(kr[:], cs[:, r], ks[:, r, 0], ALU.subtract)
                    pool.wait_ge(S["q1_ready"], u + 1)
                    nc.gpsimd.tensor_tensor(qf[:], qf[:], qs[:, r, 0], ALU.subtract).then_inc(S["rem_ready"], 1)
                if s.on(5):
                    u, uh, r = s.tile(5)
                    rstd(mv2, rs2, u, r, S["stats2"], S["rstd2_link"], S["rstd2"])
                if s.on(-1):
                    u, uh, r = s.tile(-1)
                    pool.wait_ge(S["k2q2_ready"], u + 1)
                    nc.gpsimd.tensor_tensor(ks[:, r, 2], kr[:], ks[:, r, 1], ALU.subtract)
                    nc.gpsimd.tensor_tensor(qs[:, r, 2], qf[:], qs[:, r, 1], ALU.subtract).then_inc(S["split_ready"], 1)
                if s.on(0):
                    max_parts(s, 0)
                if s.on(4):
                    u, uh, r = s.tile(4)
                    pool.wait_ge(nat_in[r], 32 * (uh + 1))
                    pool.wait_ge(rdb_in, 16 * (u + 1))
                    link = chain(pool, S["x1_link"], 1, u)
                    link(nc.gpsimd.tensor_tensor(nat[:, r], nat[:, r], rdb[:], ALU.mult))
                    nc.gpsimd.tensor_tensor(xs[:, u], xs[:, u], nat[:, r], ALU.add).then_inc(S["x1_ready"], 1)
                if s.on(6):
                    u, uh, r = s.tile(6)
                    pool.wait_ge(S["route2"], u + 1)
                    settle(pool)
                    for k in range(TOPK):
                        nc.gpsimd.indirect_dma_start(out=xd, out_offset=IndexOnAxis(slots[:, r, k:k + 1], 0),
                                                     in_=pay[:, r], in_offset=None).then_inc(sc_out[r], 16)
                if s.on(0):
                    max_parts(s, 1)
            steps(pool, body)

            def scatter(quarter, r):
                i, iq, slot, on = etile(quarter, r, 2)
                if on:
                    pool.wait_ge(S["y_copied"], i + 1)
                    settle(pool)
                    nc.gpsimd.indirect_dma_start(out=yd, out_offset=IndexOnAxis(idxc[:, slot:slot + 1], 0),
                                                 in_=ysb[:, slot], in_offset=None, bounds_check=TOPK * TOK - 1,
                                                 oob_is_err=False).then_inc(y_out[slot], 16)
            chunk_loop(pool, scatter)

        @block.scalar
        def _(act_e):
            act_e.wait_ge(S["small_in"], 80)
            nc.scalar.activation(gates[:, 0:2], gates[:, 0:2], ACT.Tanh).then_inc(S["gates_ready"], 1)
            act_e.wait_ge(S["wr_T"], 1)
            nc.scalar.copy(wr[:], HB[:, 0:HC * E].rearrange("p (c e) -> p c e", c=HC)).then_inc(S["wr_ready"], 1)

            def body(s):
                for b in range(2):
                    for j in range(HEADS):
                        if s.on(1):
                            u = s.tile(1)[0]
                            n = PAIRS * u + HEADS * b + j
                            act_e.wait_ge(S["scores_T"], n + 1)
                            wait(act_e, s, S["pv_ready"], 2 * (2 * u + b - 1) + j // 4 + 1)
                            nc.scalar.activation(prob[:, j], ST[j % 2][:], ACT.Exp, scale=SCALE).then_inc(S["exp_ready"], 1)
                        if s.on(-1) and b == 0 and j in (0, 1, 4):
                            u, uh, r = s.tile(-1)
                            if j == 0:
                                act_e.wait_ge(cs_in[r], 16 * (uh + 1))
                                wait(act_e, s, parts_out[r], 96 * uh)
                                wait(act_e, s, S["split_ready"], u)
                                nc.scalar.copy(ks[:, r, 0], cs[:, r]).then_inc(S["k1_ready"], 1)
                            if j == 1:
                                act_e.wait_ge(S["q_ready"], u + 1)
                                nc.scalar.copy(qs[:, r, 0], qf[:]).then_inc(S["q1_ready"], 1)
                            if j == 4:
                                act_e.wait_ge(S["rem_ready"], u + 1)
                                nc.scalar.copy(ks[:, r, 1], kr[:])
                                nc.scalar.copy(qs[:, r, 1], qf[:]).then_inc(S["k2q2_ready"], 1)
                        if j == 3:
                            if s.on(0) if b else s.on(1):
                                n = 2 * s.tile(0)[0] + b - 1
                                rm = (b - 1) % 2
                                slot = (2 * s.odd + b - 1) % 4
                                act_e.wait_ge(S["m_T"], n + 1)
                                wait(act_e, s, mrow_in[(slot - 2) % 4], 48 * ((s.half if 2 * s.odd + b - 1 >= 0 else s.half - 1) + (1 if slot >= 2 else 0)))
                                nc.scalar.copy(mT[:, rm], MVB[0:MB_PARTS * PAIRS, 0:P // 2].bitcast(BF16)).then_inc(S["m_T_copied"], 1)
                                act_e.wait_ge(S["m_T_copied"], n + 1)
                                for k in range(MB_PARTS):
                                    act_e.dma_start(qst[MROW + k:MROW + k + 1, slot],
                                                    mT[PAIRS * k:PAIRS * (k + 1), rm]).then_inc(mrow_in[slot], 16)
                            if s.on(1) if b else s.on(2):
                                n = 2 * s.tile(0)[0] + b - 3
                                act_e.wait_ge(S["pv_ready"], 2 * (n + 1))
                                wait(act_e, s, o_out, 16 * n)
                                nc.scalar.copy(osb[:], PV[:]).then_inc(S["o_copied"], 1)
                                act_e.wait_ge(S["o_copied"], n + 1)
                                act_e.dma_start(att_raw[bass.ds(2 * n, 2)].rearrange("a p l -> p a l"),
                                                osb[:].rearrange("p (a l) -> p a l", a=2)).then_inc(o_out, 16)
                            if b == 0 and s.on(0):
                                t, th, r = s.tile(0)
                                act_e.wait_ge(S["v_T"], t + 1)
                                wait(act_e, s, S["pv_ready"], 4 * (t - 1))
                                nc.scalar.copy(vt[:, r, :, :, 0:DH],
                                               HB[:, 0:2 * P].rearrange("p (c j v) -> p c j v", c=2, j=PAIRS)).then_inc(S["v_T_copied"], 1)
                            if b == 1 and s.on(5):
                                u = s.tile(5)[0]
                                act_e.wait_ge(S["h_T"], u + 1)
                                wait(act_e, s, S["logits"], u)
                                nc.scalar.copy(hT[:], HB[:, 0:HC * P].rearrange("p (c q) -> p c q", c=HC)).then_inc(S["h_T_copied"], 1)
            steps(act_e, body)

            act_e.wait_ge(S["wts_link"], 1)
            nc.scalar.activation(wts[:], wts[:], ACT.Exp).then_inc(S["exp_w"], 1)

            def expert_act(quarter, r):
                i, iq, slot, on = etile(quarter, r, 1)
                if on:
                    act_e.wait_ge(S["act_T"], i + 1)
                    if not isinstance(i, int) or i >= 2:
                        act_e.wait_ge(S["y_ready"], i - 1)
                    nc.scalar.copy(actT[:, slot % 2], ATB[:, 0:D]).then_inc(S["act_T_copied"], 1)
                i, iq, slot, on = etile(quarter, r, -1)
                if on:
                    act_e.wait_ge(S["x_T"], i + 1)
                    if not isinstance(i, int) or i >= 2:
                        act_e.wait_ge(S["gu_ready"], i - 1)
                    nc.scalar.copy(xT[:, slot % 2], XTB[:, 0:H]).then_inc(S["x_T_copied"], 1)
                i, iq, slot, on = etile(quarter, r, 0)
                if on:
                    act_e.wait_ge(S["gate_ready"], i + 1)
                    if not isinstance(i, int) or i >= 2:
                        act_e.wait_ge(S["act_ready"], i - 1)
                    nc.scalar.activation(glu[:, slot % 2], gub[:, slot % 2, :, 0], ACT.Sigmoid, scale=ALPHA).then_inc(S["sig_ready"], 1)
            chunk_loop(act_e, expert_act)

        @block.vector
        def _(dve):
            nc.vector.memset(PV[:], 0.0)
            dve.wait_ge(S["consts"], 1)
            dve.wait_ge(S["gates_ready"], 1)
            nc.vector.tensor_tensor(gates[:, 2:3], gates[:, 0:1], gates[:, 2:3], ALU.mult).then_inc(S["gates_ready"], 1)
            dve.wait_ge(S["gates_ready"], 2)

            def stats(src, st, mv, u, r, link_sem, done):
                link = chain(dve, link_sem, 1, u)
                link(nc.vector.bn_stats(st[:], src))
                settle(dve)
                nc.vector.bn_aggr(mv[:, r], st[:]).then_inc(done, 1)

            def route1(s):
                u, uh, r = s.tile(6)
                link = chain(dve, S["route_link"], 11, u)
                dve.wait_ge(S["logits"], u + 1)
                link(nc.vector.tensor_tensor(lg[:], RB[:, 0:E], br[:], ALU.add))
                settle(dve)
                link(nc.vector.max(best[:], lg[:]))
                nc.vector.tensor_copy(top[:, bass.ds(u, 1)], best[:].unsqueeze(1))
                link(nc.vector.max_index(tidx[:], best[:], lg[:]))
                link(nc.vector.tensor_copy(tidf[:], tidx[:, 0:TOPK]))
                link(nc.vector.tensor_tensor(hot[:], e_iota, tidf[:].unsqueeze(2).to_broadcast([P, TOPK, E]), ALU.is_equal))
                with nc.allow_low_precision("counts up to 16"):
                    link(nc.vector.tensor_reduce(pick[:, r], hot[:].rearrange("p k e -> p e k"), AX.X, ALU.add))
                nc.vector.tensor_tensor(seen[:, 1 - r], seen[:, r], pick[:, r], ALU.add).then_inc(S["route1"], 1)
                link(nc.vector.tensor_tensor(tmp[:], hot[:], k_base, ALU.mult))
                link(nc.vector.tensor_reduce(dst[:], tmp[:].rearrange("p k e -> p e k"), AX.X, ALU.add))
                link(nc.vector.tensor_scalar(pay[:, r, H:PW].bitcast(U32), dst[:], tok_f[:, bass.ds(u, 1)], None, ALU.add))
                return link

            def route2(s, link):
                u, uh, r = s.tile(6)
                dve.wait_ge(S["ranks"], u + 1)
                link(nc.vector.tensor_tensor(slot_base[:], RB[:, E:2 * E], e_region, ALU.add))
                link(nc.vector.tensor_tensor(tmp[:], hot[:], slot_base[:].unsqueeze(1).to_broadcast([P, TOPK, E]), ALU.mult))
                with nc.allow_low_precision("whole numbers under 2 ** 24"):
                    nc.vector.tensor_reduce(slots[:, r], tmp[:], AX.X, ALU.add).then_inc(S["route2"], 1)

            def body(s):
                link = None
                for b in range(2):
                    for j in range(HEADS):
                        if s.on(0):
                            t = s.tile(0)[0]
                            n = PAIRS * t + HEADS * b + j
                            dve.wait_ge(S["scores"], n + 1)
                            if j == 0:
                                wait(dve, s, S["mpart_ready"], 2 * t + b - 1)
                            nc.vector.tensor_reduce(mx[:, b, 2 * j:2 * j + 2], S1[j % 2][:].rearrange("p (c l) -> p c l", c=2),
                                                    AX.X, ALU.max).then_inc(S["max_ready"], 1)
                        if s.on(-1) and b == 0 and j == 0:
                            u, uh, r = s.tile(-1)
                            dve.wait_ge(S["x_in_first"], 16)
                            if s.loop or u > 0:
                                dve.wait_ge(S["x_in_rest"], 16)
                            stats(xs[:, u], st1, mv1, u, r, S["stats1_link"], S["stats1"])
                        if s.on(-1) and b == 0 and j == 1:
                            u, uh, r = s.tile(-1)
                            dve.wait_ge(S["rstd1"], u + 1)
                            wait(dve, s, S["split_ready"], u)
                            nc.vector.tensor_scalar(qf[:], xs[:, u], mv1[:, r, 0:1], rs1[:, r, 1:2],
                                                    ALU.subtract, ALU.mult).then_inc(S["q_ready"], 1)
                        if s.on(5) and b == 0 and j == 4:
                            u, uh, r = s.tile(5)
                            dve.wait_ge(S["rstd2"], u + 1)
                            wait(dve, s, sc_out[r], 16 * TOPK * uh)
                            nc.vector.tensor_scalar(pay[:, r, 0:H], xs[:, u], mv2[:, r, 0:1], rs2[:, r, 1:2],
                                                    ALU.subtract, ALU.mult).then_inc(S["h_ready"], 1)
                        if s.on(6) and b == 0 and j == 5:
                            link = route1(s)
                        if s.on(6) and b == 1 and j == 1:
                            route2(s, link)
                        if s.on(3) and b == 1 and j == 4:
                            u, uh, r = s.tile(3)
                            dve.wait_ge(nat_in[r], 32 * (uh + 1))
                            wait(dve, s, S["rd_out"], 16 * (u - 1))
                            rlink = chain(dve, S["pow_link"], 1, u)
                            rlink(nc.vector.reciprocal(rden[:, r], den[:, r]))
                            nc.vector.tensor_scalar(rden[:, r], rden[:, r], gates[:, 2:3], None, ALU.mult).then_inc(S["rden_ready"], 1)
                        if s.on(4) and b == 1 and j == 7:
                            u, uh, r = s.tile(4)
                            dve.wait_ge(S["x1_ready"], u + 1)
                            stats(xs[:, u], st2, mv2, u, r, S["stats2_link"], S["stats2"])
            steps(dve, body)

            link = chain(dve, S["table_link"], 20, 0)
            dve.wait_ge(S["counts"], 1)
            link(nc.vector.tensor_copy(cnt[:, 0], RB[0:1, 0:E]))
            link(nc.vector.tensor_scalar(cnti[:, 0], cnt[:, 0], float(P - 1), None, ALU.add))
            link(nc.vector.tensor_scalar(cnti[:, 1], cnti[:, 0], 7, None, ALU.arith_shift_right))
            link(nc.vector.tensor_copy(cnt[:, 1], cnti[:, 1]))
            link(nc.vector.tensor_copy(cnt[:, 2:6], cnt[:, 1:2].to_broadcast([1, 4, E])))
            src = 1
            for n, by in enumerate((1, 2, 4, 8)):
                link(nc.vector.tensor_copy(cnt[:, 2 + n, 0:by], cnt[:, src, 0:by]))
                link(nc.vector.tensor_tensor(cnt[:, 2 + n, by:E], cnt[:, src, by:E], cnt[:, src, 0:E - by], ALU.add))
                src = 2 + n
            ends = cnt[:, src]
            nc.vector.tensor_tensor(padrow[:], cnt[:, 0], e_region[0:1], ALU.add)
            link(nc.vector.tensor_tensor(cmp[:], ends.unsqueeze(1).to_broadcast([1, MT, E]),
                                         tile_f[:].unsqueeze(2).to_broadcast([1, MT, E]), ALU.is_le))
            link(nc.vector.tensor_tensor(cmpn[:], cmp[:], cnt[:, 1].unsqueeze(1).to_broadcast([1, MT, E]), ALU.mult))
            nc.vector.tensor_reduce(tabf[:, 0], cmp[:], AX.X, ALU.add)
            link(nc.vector.tensor_reduce(tabf[:, 1], cmpn[:], AX.X, ALU.add))
            nc.vector.tensor_scalar(tabf[:, 2], tabf[:, 0], float(E), float(P), ALU.is_lt, ALU.mult)
            link(nc.vector.tensor_tensor(tabf[:, 3], tile_f[:], tabf[:, 1], ALU.subtract))
            link(nc.vector.tensor_tensor(tabf[:, 4], tabf[:, 3], tabf[:, 2], ALU.mult))
            link(nc.vector.scalar_tensor_tensor(tab[:, 0], tabf[:, 0], float(REGION), tabf[:, 4], ALU.mult, ALU.add))
            nc.vector.tensor_scalar(tab[:, 1], tabf[:, 0], float(E - 1), None, ALU.min).then_inc(S["table_ready"], 1)
            wlink = chain(dve, S["wts_link"], 4, 0)
            wlink(nc.vector.tensor_tensor(wts[:], top[:, :, 0:TOPK], top[:, :, 0:1].to_broadcast([P, NT, TOPK]), ALU.subtract))
            dve.wait_ge(S["exp_w"], 1)
            wlink(nc.vector.tensor_reduce(wsum[:], wts[:], AX.X, ALU.add))
            wlink(nc.vector.reciprocal(wsum[:], wsum[:]))
            wlink(nc.vector.tensor_scalar(wsum[:], wsum[:], gates[:, 1:2], None, ALU.mult))
            nc.vector.tensor_tensor(wts[:], wts[:], wsum[:].unsqueeze(2).to_broadcast([P, NT, TOPK]), ALU.mult).then_inc(S["wts_ready"], 1)
            dve.wait_ge(S["table_ready"], 1)
            dve.wait_ge(S["bias_in"], 32)

            experts = {}

            def expert_dve(quarter, r):
                i, iq, slot, on = etile(quarter, r, 0)
                gate, up = gub[:, slot % 2, :, 0], gub[:, slot % 2, :, 1]
                if on:
                    e = dve.value_load(tab[0:1, 1, bass.ds(i, 1)], min_val=0, max_val=E - 1)
                    dve.wait_ge(xt_in[slot], 16 * (iq + 1))
                    if not isinstance(i, int) or i >= 4:
                        dve.wait_ge(y_out[slot], 16 * iq)
                    nc.vector.tensor_copy(idxc[:, slot:slot + 1], xt[:, slot, bass.ds(e + H, 1)].bitcast(U32)).then_inc(S["dest_ready"], 1)
                    dve.wait_ge(S["gu_ready"], i + 1)
                    link = chain(dve, S["act_link"], 2, i)
                    link(nc.vector.tensor_tensor(gub[:, slot % 2].rearrange("p f two -> p (f two)"), GU[slot % 2][:],
                                                 bias_gu[:, e], ALU.add))
                    nc.vector.tensor_scalar(gate, gate, LIMIT, None, ALU.min).then_inc(S["gate_ready"], 1)
                    nc.vector.tensor_scalar(up, up, LIMIT, -LIMIT, ALU.min, ALU.max)
                j, jq, jslot, jon = etile(quarter, r, 2)
                if jon:
                    ej = dve.value_load(tab[0:1, 1, bass.ds(j, 1)], min_val=0, max_val=E - 1)
                    dve.wait_ge(S["y_ready"], j + 1)
                    if not isinstance(j, int) or j >= 4:
                        dve.wait_ge(y_out[jslot], 16 * jq)
                    nc.vector.tensor_tensor(ysb[:, jslot], YB[jslot % 2][:, 0:H], bias_dn[:, ej], ALU.add).then_inc(S["y_copied"], 1)
                if on:
                    dve.wait_ge(S["sig_ready"], i + 1)
                    link(nc.vector.tensor_tensor(glu[:, slot % 2], gate, glu[:, slot % 2], ALU.mult))
                    if not isinstance(i, int) or i >= 2:
                        dve.wait_ge(S["act_T"], i - 1)
                    nc.vector.scalar_tensor_tensor(act[:, slot % 2], up, 1.0, glu[:, slot % 2], ALU.add, ALU.mult).then_inc(S["act_ready"], 1)
            chunk_loop(dve, expert_dve)

            for u in range(NT):
                dve.wait_ge(yk_in[u % 2], 16 * (u // 2 + 1))
                if u >= 2:
                    dve.wait_ge(fin_out[u % 2], 16 * (u // 2))
                link = chain(dve, S["sum_link"], TOPK - 1, u)
                for k in range(TOPK):
                    acc = xs[:, u] if k == 0 else fin[:, u % 2]
                    ins = nc.vector.scalar_tensor_tensor(fin[:, u % 2], yk[:, u % 2, k], wts[:, u, k:k + 1], acc, ALU.mult, ALU.add)
                    if k < TOPK - 1:
                        link(ins)
                    else:
                        ins.then_inc(S["fin_ready"], 1)

        @block.tensor
        def _(pe):
            pe.wait_ge(S["consts"], 1)
            pe.wait_ge(S["small_in"], 80)
            for c in range(HC):
                ins = nc.tensor.transpose(HB[:, c * E:(c + 1) * E], wr_nat[:, c * P:(c + 1) * P], ident[0:E, 0:E])
            ins.then_inc(S["wr_T"], 1)
            pe.wait_ge(S["wr_ready"], 1)

            def value_product(s, n, lag, b, quad):
                u, uh, r = s.tile(lag)
                pe.wait_ge(S["exp_ready"], HEADS * n + 4 * quad + 4)
                if quad == 0:
                    wait(pe, s, S["o_copied"], n)
                    pe.wait_ge(S["v_T_copied"], u + 1)
                for c in range(2):
                    for jj in range(4):
                        j = 4 * quad + jj
                        ins = nc.tensor.matmul(PV[32 * jj:32 * jj + 2 * DH, quad * L:(quad + 1) * L],
                                               vt[:, r, c, HEADS * b + j], prob[:, j, c * L:(c + 1) * L],
                                               start=(c == 0), stop=(c == 1))
                ins.then_inc(S["pv_ready"], 1)

            def body(s):
                if s.on(0):
                    t, th, r = s.tile(0)
                    pe.wait_ge(cv_in[r], 16 * (th + 1))
                    wait(pe, s, S["h_T_copied"], t - 5)
                    for c in range(2):
                        ins = nc.tensor.transpose(HB[:, c * P:(c + 1) * P], cv[:, r, c * P:(c + 1) * P], ident[:])
                    ins.then_inc(S["v_T"], 1)
                if s.on(6):
                    u = s.tile(6)[0]
                    wait(pe, s, S["route2"], u)
                    pe.wait_ge(S["h_T_copied"], u + 1)
                    for c in range(HC):
                        ins = nc.tensor.matmul(RB[:, 0:E], hT[:, c], wr[:, c], start=(c == 0), stop=(c == HC - 1))
                    ins.then_inc(S["logits"], 1)
                for b in range(2):
                    for quad in range(2):
                        for j in range(4 * quad, 4 * quad + 4):
                            if s.on(1):
                                u, uh, r = s.tile(1)
                                slot = 2 * r + b
                                n = PAIRS * u + HEADS * b + j
                                if j == 0:
                                    pe.wait_ge(mrow_in[slot], 48 * (uh + 1))
                                wait(pe, s, S["exp_ready"], n - 1)
                                for c in range(2):
                                    ins = nc.tensor.matmul(ST[j % 2][:, c * L:(c + 1) * L],
                                                           kst[0:MROW + 3, slot, j, c * P:(c + 1) * P],
                                                           qst[0:MROW + 3, slot, j], start=True, stop=True)
                                ins.then_inc(S["scores_T"], 1)
                            if s.on(0):
                                t, th, r = s.tile(0)
                                slot = 2 * r + b
                                n = PAIRS * t + HEADS * b + j
                                if j == 0:
                                    pe.wait_ge(stk_in[slot], 128 * (th + 1))
                                wait(pe, s, S["max_ready"], n - 1)
                                for c in range(2):
                                    ins = nc.tensor.matmul(S1[j % 2][:, c * L:(c + 1) * L],
                                                           qst[0:MROW, slot, j, c * P:(c + 1) * P],
                                                           kst[0:MROW, slot, j], start=True, stop=True)
                                ins.then_inc(S["scores"], 1)
                        t = s.tile(0)[0]
                        if quad == 0:
                            if s.on(0) if b else s.on(1):
                                n = 2 * t + b - 1
                                pe.wait_ge(S["mpart_ready"], n + 1)
                                wait(pe, s, S["m_T_copied"], n)
                                settle(pe)
                                nc.tensor.transpose(MVB[0:MB_PARTS * PAIRS, 0:P // 2].bitcast(BF16),
                                                    mpart[:, (b - 1) % 2].rearrange("p s j -> p (s j)"),
                                                    identb[:]).then_inc(S["m_T"], 1)
                            lag = 1 if b else 2
                            if s.on(lag):
                                value_product(s, 2 * t + b - 3, lag, (b - 3) % 2, 1)
                        elif s.on(1):
                            value_product(s, 2 * t + b - 2, 1, b, 0)
                    if b == 0 and s.on(6):
                        u, uh, r = s.tile(6)
                        pe.wait_ge(S["route1"], u + 1)
                        nc.tensor.matmul(RB[:, E:2 * E], before[:], pick[:, r], start=True, stop=False)
                        nc.tensor.matmul(RB[:, E:2 * E], ones[:], seen[:, r], start=False, stop=True).then_inc(S["ranks"], 1)
                    if b == 0 and s.on(5):
                        u = s.tile(5)[0]
                        pe.wait_ge(S["h_ready"], u + 1)
                        if s.on(0):
                            pe.wait_ge(S["v_T_copied"], t + 1)
                        else:
                            pe.wait_ge(S["v_T_copied"], NT)
                            wait(pe, s, S["h_T_copied"], u)
                        for c in range(HC):
                            ins = nc.tensor.transpose(HB[:, c * P:(c + 1) * P], pay[:, s.tile(5)[2], c * P:(c + 1) * P], ident[:])
                        ins.then_inc(S["h_T"], 1)
            steps(pe, body)

            pe.wait_ge(S["route2"], NT)
            nc.tensor.matmul(RB[:, 0:E], ones[:], seen[:, NT % 2], start=True, stop=True).then_inc(S["counts"], 1)
            pe.wait_ge(S["table_ready"], 1)
            pe.wait_ge(S["w_in"], 32 * E)

            def expert_pe(quarter, r):
                i, iq, slot, on = etile(quarter, r, 0)
                if on:
                    e = pe.value_load(tab[0:1, 1, bass.ds(i, 1)], min_val=0, max_val=E - 1)
                    pe.wait_ge(S["x_T_copied"], i + 1)
                    if not isinstance(i, int) or i >= 2:
                        pe.wait_ge(S["gate_ready"], i - 1)
                    for c in range(HC):
                        ins = nc.tensor.matmul(GU[slot % 2][:], xT[:, slot % 2, c * P:(c + 1) * P], wgu[:, e, c],
                                               start=(c == 0), stop=(c == HC - 1))
                    ins.then_inc(S["gu_ready"], 1)
                i, iq, slot, on = etile(quarter, r, 1)
                if on:
                    pe.wait_ge(S["act_ready"], i + 1)
                    if not isinstance(i, int) or i >= 1:
                        pe.wait_ge(S["act_T_copied"], i)
                    for c in range(HC):
                        ins = nc.tensor.transpose(ATB[:, c * P:(c + 1) * P], act[:, slot % 2, c * P:(c + 1) * P], ident[:])
                    ins.then_inc(S["act_T"], 1)
                i, iq, slot, on = etile(quarter, r, -1)
                if on:
                    pe.wait_ge(xt_in[slot], 16 * (iq + 1))
                    if not isinstance(i, int) or i >= 1:
                        pe.wait_ge(S["x_T_copied"], i)
                    for c in range(HC):
                        ins = nc.tensor.transpose(XTB[:, c * P:(c + 1) * P], xt[:, slot, c * P:(c + 1) * P], ident[:])
                    ins.then_inc(S["x_T"], 1)
                i, iq, slot, on = etile(quarter, r, 2)
                if on:
                    e = pe.value_load(tab[0:1, 1, bass.ds(i, 1)], min_val=0, max_val=E - 1)
                    pe.wait_ge(S["act_T_copied"], i + 1)
                    if not isinstance(i, int) or i >= 2:
                        pe.wait_ge(S["y_copied"], i - 1)
                    for c in range(HC):
                        ins = nc.tensor.matmul(YB[slot % 2][:, 0:H], actT[:, slot % 2, c * P:(c + 1) * P], wdn[:, e, c],
                                               start=(c == 0), stop=(c == HC - 1))
                    ins.then_inc(S["y_ready"], 1)
            chunk_loop(pe, expert_pe)


_INS = ["x", "ctx_2048", "g_xattn", "g_ffn", "L0_xattn_gamma", "L0_ffn_router_weight", "L0_ffn_router_bias",
        "L0_ffn_gate_up_proj", "L0_ffn_gate_up_proj_bias", "L0_ffn_down_proj", "L0_ffn_down_proj_bias"]


def kernel(**inputs):
    import numpy as np
    import concourse.bacc as bacc
    from concourse.bass_utils import run_bass_kernel_spmd

    nc = bacc.Bacc("TRN2", target_bir_lowering=False, num_devices=1)
    arrays, args = {}, []
    for name in _INS:
        a = np.ascontiguousarray(inputs[name])
        if a.ndim == 0:
            a = a.reshape(1, 1)
        arrays[f"in_{name}"] = a
        args.append(nc.dram_tensor(f"in_{name}", a.shape, mybir.dt.from_np(a.dtype), kind="ExternalInput").ap())
    out = nc.dram_tensor("out_x", inputs["x"].shape, F32, kind="ExternalOutput").ap()
    flamingo_gated_kernel(nc, *args, out)
    r = run_bass_kernel_spmd(nc, [arrays], core_ids=[0])
    return r.results[0]["out_x"]
```

```python
from contextlib import ExitStack

import concourse.bass as bass
from concourse import mybir

F32 = mybir.dt.float32
BF16 = mybir.dt.bfloat16
U32 = mybir.dt.uint32
I32 = mybir.dt.int32
ALU = mybir.AluOpType
ACT = mybir.ActivationFunctionType
AX = mybir.AxisListType
IndexOnAxis = bass.IndirectOffsetOnAxis

P = 128
EPS = 1e-5
ALPHA = 1.702
LIMIT = 7.0
HEADS = 8
TOPK = 4
MROW = 96
MB_PARTS = 3


def flamingo_gated_kernel(nc, x, ctx_in, g_xattn, g_ffn, gamma, router_w, router_b,
                          gate_up, gate_up_b, down, down_b, out):
    NB, CH, L = x.shape
    DH = CH // HEADS
    E, H, F2 = gate_up.shape
    D = F2 // 2
    TOK = NB * CH
    NT = TOK // P
    PAIRS = 2 * HEADS
    HC = H // P
    SCALE = float(DH) ** -0.5
    NPROD = 6
    STK = NPROD * DH
    REGION = TOK + P
    ROWS = E * REGION + P
    PW = H + E
    MT = TOK * TOPK // P + E
    SKIP = 2 * TOK * TOPK
    assert (P, L, MT % 4) == (2 * CH, H, 0)

    x_rows = x.rearrange("b c l -> (b c) l")
    ctx_rows = ctx_in.rearrange("b c l -> (b c) l")
    out_rows = out.rearrange("b c l -> (b c) l")

    stacks = nc.dram_tensor("stacks", [NT, 2 * NPROD, P, L], BF16, kind="Internal").ap()
    att_raw = nc.dram_tensor("att_raw", [NB * 2, P, L], F32, kind="Internal").ap()
    rden_dram = nc.dram_tensor("rden_dram", [NB * HEADS, L], F32, kind="Internal").ap()
    xd = nc.dram_tensor("xd", [ROWS, PW], F32, kind="Internal").ap()
    yd = nc.dram_tensor("yd", [TOPK * TOK, H], F32, kind="Internal").ap()

    with ExitStack() as stack:
        def sb(name, shape, dt):
            return stack.enter_context(nc.sbuf_tensor(name, shape, dt))

        def sem(name):
            return stack.enter_context(nc.semaphore(name))

        bank = [stack.enter_context(nc.psum_tensor(f"bank{i}", [P, 512], F32)) for i in range(8)]
        S1, ST = bank[0:2], bank[2:4]
        PV, MVB, HB, RB = bank[4:8]
        GU, XTB, ATB, YB = bank[0:2], bank[2], bank[3], bank[4:6]

        wgu = sb("wgu", [P, E, HC, F2], F32)
        wdn = sb("wdn", [P, E, HC, H], F32)
        xs = sb("xs", [P, NT, L], F32)
        area = sb("area", [P, 3 * 4096], F32)
        cs = area[:, 0:512].rearrange("p (s l) -> p s l", s=2)
        cv = area[:, 512:1024].rearrange("p (s l) -> p s l", s=2)
        stk = area[:, 4096:12288].bitcast(BF16).rearrange("p (s two j l) -> p s two j l", s=4, two=2, j=HEADS)
        bias_gu = area[:, 0:E * F2].rearrange("p (e f) -> p e f", e=E)
        bias_dn = area[:, E * F2:E * F2 + E * H].rearrange("p (e f) -> p e f", e=E)
        work = sb("work", [P, 7680], F32)
        prob = work[:, 0:4096].rearrange("p (s l) -> p s l", s=HEADS)
        vt = work[:, 4096:5120].rearrange("p (s c j v) -> p s c j v", s=2, c=2, j=PAIRS)
        osb = work[:, 5120:5632]
        qf = work[:, 5632:5888]
        kr = work[:, 5888:6144]
        parts = work[:, 6144:7680].bitcast(BF16).rearrange("p (s n l) -> p s n l", s=2, n=2 * MB_PARTS)
        Q3, Q2, Q1, K1, K2, K3 = range(6)
        xt = work[:, 0:4 * PW].rearrange("p (s f) -> p s f", s=4)
        o = 4 * PW
        ysb = work[:, o:o + 4 * H].rearrange("p (s f) -> p s f", s=4)
        o += 4 * H
        xT = work[:, o:o + 2 * H].rearrange("p (s f) -> p s f", s=2)
        o += 2 * H
        actT = work[:, o:o + 2 * D].rearrange("p (s f) -> p s f", s=2)
        o += 2 * D
        gub = work[:, o:o + 2 * F2].rearrange("p (s f two) -> p s f two", s=2, two=2)
        o += 2 * F2
        glu = work[:, o:o + 2 * D].rearrange("p (s f) -> p s f", s=2)
        o += 2 * D
        act = work[:, o:o + 2 * D].rearrange("p (s f) -> p s f", s=2)
        assert o + 2 * D <= 7680
        yk = area[:, 0:2 * TOPK * H].rearrange("p (s k f) -> p s k f", s=2, k=TOPK)
        fin = area[:, 2048:2048 + 2 * H].rearrange("p (s f) -> p s f", s=2)

        st1 = sb("st1", [P, 6], F32)
        mv1 = sb("mv1", [P, 2, 2], F32)
        rs1 = sb("rs1", [P, 2, 2], F32)
        st2 = sb("st2", [P, 6], F32)
        mv2 = sb("mv2", [P, 2, 2], F32)
        rs2 = sb("rs2", [P, 2, 2], F32)
        mx = sb("mx", [P, 2, PAIRS], F32)
        mrem = sb("mrem", [P, 2, PAIRS], F32)
        mpart = sb("mpart", [P, 2, MB_PARTS, PAIRS], BF16)
        mT = sb("mT", [MB_PARTS * PAIRS, 2, P], BF16)
        nat = sb("nat", [P, 2, L], F32)
        den = sb("den", [P, 2, 32], F32)
        rden = sb("rden", [P, 2, 32], F32)
        rdb = sb("rdb", [P, L], F32)
        pay = sb("pay", [P, 2, PW], F32)
        hT = sb("hT", [P, HC, P], F32)
        zpay = sb("zpay", [P, PW], F32)
        wr = sb("wr", [P, HC, E], F32)
        wr_nat = sb("wr_nat", [E, H], F32)
        br = sb("br", [P, E], F32)
        lg = sb("lg", [P, E], F32)
        top = sb("top", [P, NT, 8], F32)
        best = sb("best", [P, 8], F32)
        tidx = sb("tidx", [P, 8], U32)
        tidf = sb("tidf", [P, TOPK], F32)
        hot = sb("hot", [P, TOPK, E], F32)
        tmp = sb("tmp", [P, TOPK, E], F32)
        dst = sb("dst", [P, E], F32)
        pick = sb("pick", [P, 2, E], BF16)
        seen = sb("seen", [P, 2, E], BF16)
        slot_base = sb("slot_base", [P, E], F32)
        slots = sb("slots", [P, 2, TOPK], U32)
        wts = sb("wts", [P, NT, TOPK], F32)
        wsum = sb("wsum", [P, NT], F32)
        gates = sb("gates", [P, 3], F32)
        ident = sb("ident", [P, P], F32)
        identb = sb("identb", [P, P], BF16)
        before = sb("before", [P, P], BF16)
        ones = sb("ones", [P, P], BF16)
        minus_half = sb("minus_half", [P, 1], F32)
        iota_i = work[:, 0:3 * TOPK * E].bitcast(I32).rearrange("p (n k e) -> p n k e", n=3, k=TOPK)
        iota_f = sb("iota_f", [P, 3, TOPK, E], F32)
        e_iota, k_base, e_region = iota_f[:, 0], iota_f[:, 1], iota_f[:, 2, 0]
        tok_i = sb("tok_i", [P, NT], I32)
        tok_f = sb("tok_f", [P, NT], F32)
        tile_i = sb("tile_i", [1, MT], I32)
        tile_f = sb("tile_f", [1, MT], F32)
        cnt = sb("cnt", [1, 8, E], F32)
        cnti = sb("cnti", [1, 2, E], I32)
        cmp = work[0:1, 0:MT * E].rearrange("p (i e) -> p i e", e=E)
        cmpn = work[0:1, MT * E:2 * MT * E].rearrange("p (i e) -> p i e", e=E)
        tabf = sb("tabf", [1, 6, MT], F32)
        tab = sb("tab", [1, 2, MT], I32)
        padrow = sb("padrow", [1, E], I32)
        idxc = sb("idxc", [P, 4], U32)

        names = """passed x_in small_in w_in bias_in consts gates_ready wr_T wr_ready
            stats1 rstd1 q_ready k1_ready q1_ready rem_ready k2q2_ready split_ready stats1_link rstd1_link
            scores scores_T max_ready exp_ready pv_ready mpart_ready mpart_link m_T m_T_copied
            v_T v_T_copied o_copied rden_ready x1_ready x1_link stats2 stats2_link rstd2 rstd2_link h_ready h_T
            h_T_copied logits route_link route1 ranks route2 scattered counts table_link table_ready pads_in
            x_T x_T_copied gu_ready act_T act_T_copied y_ready y_copied biased gate_ready sig_ready act_link
            act_ready dest_ready wts_link wts_ready exp_w fin_ready rd_out zero_in setup_link sum_link pow_link""".split()
        S = {n: sem(n) for n in names}
        parts_out = [sem(f"parts_out{i}") for i in range(2)]
        stk_in = [sem(f"stk_in{i}") for i in range(4)]
        mrow_in = [sem(f"mrow_in{i}") for i in range(4)]
        cs_in = [sem(f"cs_in{i}") for i in range(2)]
        cv_in = [sem(f"cv_in{i}") for i in range(2)]
        o_out = sem("o_out")
        nat_in = [sem(f"nat_in{i}") for i in range(2)]
        rdb_in = sem("rdb_in")
        sc_out = [sem(f"sc_out{i}") for i in range(2)]
        xt_in = [sem(f"xt_in{i}") for i in range(4)]
        y_out = [sem(f"y_out{i}") for i in range(4)]
        yk_in = [sem(f"yk_in{i}") for i in range(2)]
        fin_out = [sem(f"fin_out{i}") for i in range(2)]

        class Step:
            def __init__(self, half, odd):
                self.half, self.odd, self.loop = half, odd, not isinstance(half, int)

            def on(self, lag):
                return self.loop or 0 <= 2 * self.half + self.odd - lag < NT

            def tile(self, lag):
                a, odd = divmod(self.odd - lag, 2)
                return 2 * self.half + 2 * a + odd, self.half + a, odd

            def least(self, v, small):
                return self.loop or v >= small

        LAST = NT + 5

        def steps(eng, body):
            for t in range(-2, 6):
                body(Step(t // 2, t % 2))
            with eng.Fori(3, 7) as half:
                body(Step(half, 0))
                body(Step(half, 1))
            for t in range(14, LAST):
                body(Step(t // 2, t % 2))

        def wait(eng, step, s, v):
            if step.least(v, 1):
                eng.wait_ge(s, v)

        def settle(eng):
            eng.sem_inc(S["passed"], 1)

        def chain(eng, s, per, u):
            count = [0]

            def link(ins):
                count[0] += 1
                assert count[0] <= per
                ins.then_inc(s, 1)
                eng.wait_ge(s, u * per + count[0])
            return link

        def chunk_loop(eng, body):
            for i in range(-1, 4):
                body(i // 4, i % 4)
            with eng.Fori(1, MT // 4 - 1) as quarter:
                for r in range(4):
                    body(quarter, r)
            for i in range(MT - 4, MT + 2):
                body(i // 4, i % 4)

        def etile(quarter, r, lag):
            a, slot = divmod(r - lag, 4)
            i = 4 * quarter + 4 * a + slot
            return i, quarter + a, slot, (not isinstance(i, int)) or 0 <= i < MT

        block = stack.enter_context(nc.Block())

        @block.sync
        def _(sp):
            def tile_rows(rows, u):
                return rows[bass.ds(P * u, P)].rearrange("(a d) l -> d a l", d=DH)

            sp.dma_start(xs[:, 0], tile_rows(x_rows, 0)).then_inc(S["x_in"], 16)
            sp.dma_start(gates[:, 0:1], g_xattn.rearrange("(a b) -> a b", a=1).to_broadcast([P, 1])).then_inc(S["small_in"], 16)
            sp.dma_start(gates[:, 1:2], g_ffn.rearrange("(a b) -> a b", a=1).to_broadcast([P, 1])).then_inc(S["small_in"], 16)
            sp.dma_start(gates[:, 2:3], gamma.to_broadcast([P, 1])).then_inc(S["small_in"], 16)
            sp.dma_start(br[:], router_b.rearrange("(a e) -> a e", a=1).to_broadcast([P, E])).then_inc(S["small_in"], 16)
            sp.dma_start(wr_nat[:], router_w).then_inc(S["small_in"], 16)

            def stack_read(s, u, uh, r, b):
                sp.wait_ge(parts_out[r], 48 * (uh + 1))
                settle(sp)
                wait(sp, s, S["scores_T"], PAIRS * (u - 2) + HEADS * (b + 1))
                settle(sp)
                src = stacks[bass.ds(u, 1)].rearrange("o (two i) (d a) l -> (o i d) two a l", two=2, a=PAIRS)
                slot = 2 * r + b
                sp.dma_start(stk[0:STK, slot], src[:, :, HEADS * b:HEADS * (b + 1)]).then_inc(stk_in[slot], 16)

            def max_rows(s, b):
                n = 2 * s.tile(0)[0] + b - 1
                slot = (2 * s.odd + b - 1) % 4
                sp.wait_ge(S["m_T_copied"], n + 1)
                sp.dma_start(stk[MROW:MROW + MB_PARTS, slot, 0], mT[:, (b - 1) % 2]).then_inc(mrow_in[slot], 16)

            def sums_out(s, b):
                n = 2 * s.tile(0)[0] + b - 3
                sp.wait_ge(S["o_copied"], n + 1)
                settle(sp)
                sp.dma_start(att_raw[bass.ds(2 * n, 2)].rearrange("a p l -> p a l"),
                             osb[:].rearrange("p (a l) -> p a l", a=2)).then_inc(o_out, 16)

            def body(s):
                if s.on(3):
                    u, uh, r = s.tile(3)
                    sp.wait_ge(S["rden_ready"], u + 1)
                    settle(sp)
                    to = rden_dram[bass.ds(16 * u, 16)].rearrange("a (s i) -> (a s) i", s=8)
                    sp.dma_start(to, rden[:, r]).then_inc(S["rd_out"], 16)
                if s.on(0):
                    stack_read(s, *s.tile(0), 1)
                if s.on(-2):
                    u, uh, r = s.tile(-2)
                    wait(sp, s, S["rem_ready"], u - 1)
                    settle(sp)
                    sp.dma_start(cs[:, r], tile_rows(ctx_rows, u)).then_inc(cs_in[r], 16)
                if s.on(-1):
                    u, uh, r = s.tile(-1)
                    wait(sp, s, S["v_T"], u - 1)
                    settle(sp)
                    sp.dma_start(cv[:, r], ctx_rows[bass.ds(P * u, P)]).then_inc(cv_in[r], 16)
                    sp.wait_ge(S["split_ready"], u + 1)
                    settle(sp)
                    to = stacks[bass.ds(u, 1)].rearrange("o n p l -> p (o n) l")
                    for first, step, part, n in ((1, 2, Q3, 6), (2, 4, Q1, 3), (0, 4, Q2, 3)):
                        sp.dma_start(to[:, first:first + step * (n - 1) + 1:step],
                                     parts[:, r, part:part + n]).then_inc(parts_out[r], 16)
                if not s.loop and 2 * s.half + s.odd == -1:
                    for t in range(1, NT):
                        sp.dma_start(xs[:, t], tile_rows(x_rows, t)).then_inc(S["x_in"], 16)
                if s.on(0):
                    t = s.tile(0)[0]
                    sp.dma_start(wgu[:, t], gate_up[t].rearrange("(c p) f -> p c f", p=P)).then_inc(S["w_in"], 16)
                if s.on(1):
                    max_rows(s, 0)
                if s.on(2):
                    sums_out(s, 0)
                if s.on(3):
                    u, uh, r = s.tile(3)
                    sp.wait_ge(S["rd_out"], 16 * (u + 1))
                    settle(sp)
                    wait(sp, s, S["x1_ready"], u)
                    settle(sp)
                    src = rden_dram[bass.ds(16 * u, 16)].unsqueeze(0).to_broadcast([DH, 16, L])
                    sp.dma_start(rdb[:], src).then_inc(rdb_in, 16)
                if s.on(-1):
                    stack_read(s, *s.tile(-1), 0)
                if s.on(2):
                    u, uh, r = s.tile(2)
                    sp.wait_ge(o_out, 32 * (u + 1))
                    settle(sp)
                    src = att_raw[bass.ds(4 * u, 4)].rearrange("a (j r) l -> r (a j) l", r=32)
                    wait(sp, s, S["rden_ready"], u - 1)
                    settle(sp)
                    sp.dma_start(den[:, r], src[DH].rearrange("a (s i) -> a s i", s=8)).then_inc(nat_in[r], 16)
                    wait(sp, s, S["x1_ready"], u - 1)
                    settle(sp)
                    sp.dma_start(nat[:, r], src[0:DH]).then_inc(nat_in[r], 16)
                if s.on(0):
                    max_rows(s, 1)
                if s.on(1):
                    sums_out(s, 1)
                if s.on(0):
                    t = s.tile(0)[0]
                    sp.dma_start(wdn[:, t], down[t].rearrange("(c p) f -> p c f", p=P)).then_inc(S["w_in"], 16)
                if not s.loop and 2 * s.half + s.odd == NT + 1:
                    sp.wait_ge(S["scores_T"], NT * PAIRS)
                    sp.dma_start(bias_gu, gate_up_b.unsqueeze(0).to_broadcast([P, E, F2])).then_inc(S["bias_in"], 16)
                    sp.dma_start(bias_dn, down_b.unsqueeze(0).to_broadcast([P, E, H])).then_inc(S["bias_in"], 16)

            sp.wait_ge(S["consts"], 1)
            sp.dma_start(xd[E * REGION:ROWS], zpay[:]).then_inc(S["zero_in"], 16)
            steps(sp, body)

            sp.wait_ge(S["table_ready"], 1)
            with sp.Fori(0, E) as e:
                row = sp.value_load(padrow[0:1, bass.ds(e, 1)], min_val=0, max_val=E * REGION - P)
                sp.dma_start(xd[bass.ds(row, P)], zpay[:]).then_inc(S["pads_in"], 16)
            sp.wait_ge(S["pads_in"], 16 * E)
            sp.wait_ge(S["zero_in"], 16)
            for r in range(2):
                sp.wait_ge(sc_out[r], 16 * TOPK * NT // 2)

            def expert_loads(quarter, r):
                i, iq, slot, on = etile(quarter, r, -1)
                if on:
                    if not isinstance(iq, int) or iq >= 1:
                        sp.wait_ge(S["x_T"], i - 3)
                        sp.wait_ge(S["dest_ready"], i - 3)
                    row = sp.value_load(tab[0:1, 0, bass.ds(i, 1)], min_val=0, max_val=ROWS - P)
                    sp.dma_start(xt[:, slot], xd[bass.ds(row, P)]).then_inc(xt_in[slot], 16)
            chunk_loop(sp, expert_loads)

            for r in range(4):
                sp.wait_ge(y_out[r], 16 * (MT // 4))
            yv = yd.rearrange("(k t p) f -> t p k f", k=TOPK, p=P)
            for u in range(NT + 1):
                if u < NT:
                    if u >= 2:
                        sp.wait_ge(S["fin_ready"], u - 1)
                    sp.dma_start(yk[:, u % 2], yv[u]).then_inc(yk_in[u % 2], 16)
                if u >= 1:
                    sp.wait_ge(S["fin_ready"], u)
                    sp.dma_start(tile_rows(out_rows, u - 1), fin[:, (u - 1) % 2]).then_inc(fin_out[(u - 1) % 2], 16)
            for r in range(2):
                sp.wait_ge(fin_out[r], 16 * (NT // 2))

        @block.gpsimd
        def _(pool):
            link = chain(pool, S["setup_link"], 12, 0)
            link(nc.gpsimd.memset(zpay[:, 0:H], 0.0))
            link(nc.gpsimd.memset(zpay[:, H:PW].bitcast(U32), SKIP))
            link(nc.gpsimd.memset(stk[:, :, 0], 0.0))
            link(nc.gpsimd.memset(stk[:, :, 1], -1.0))
            link(nc.gpsimd.memset(ident[:], 0.0))
            link(nc.gpsimd.affine_select(out=ident[:], in_=ident[:], compare_op=ALU.not_equal, fill=1.0, base=0,
                                         pattern=[[-1, P]], channel_multiplier=1))
            link(nc.gpsimd.tensor_copy(identb[:], ident[:]))
            link(nc.gpsimd.memset(ones[:], 1.0))
            link(nc.gpsimd.affine_select(out=before[:], in_=ones[:], compare_op=ALU.is_gt, fill=0.0, base=0,
                                         pattern=[[1, P]], channel_multiplier=-1))
            nc.gpsimd.memset(minus_half[:], -0.5)
            nc.gpsimd.memset(vt[:, :, :, :, DH:2 * DH], 1.0)
            nc.gpsimd.memset(seen[:], 0.0)
            nc.gpsimd.iota(iota_i[:, 0], pattern=[[0, TOPK], [1, E]], base=0, channel_multiplier=0)
            nc.gpsimd.iota(iota_i[:, 1], pattern=[[TOK, TOPK], [0, E]], base=0, channel_multiplier=0)
            nc.gpsimd.iota(iota_i[:, 2], pattern=[[0, TOPK], [REGION, E]], base=0, channel_multiplier=0)
            nc.gpsimd.iota(tile_i[:], pattern=[[1, MT]], base=0, channel_multiplier=0)
            link(nc.gpsimd.iota(tok_i[:], pattern=[[P, NT]], base=0, channel_multiplier=1))
            nc.gpsimd.tensor_copy(iota_f[:], iota_i[:])
            nc.gpsimd.tensor_copy(tile_f[:], tile_i[:])
            link(nc.gpsimd.tensor_copy(tok_f[:], tok_i[:]))
            nc.gpsimd.tensor_copy(tok_f[:], tok_f[:]).then_inc(S["consts"], 1)

            def rstd(mv, rs, u, r, got, link_sem, done):
                pool.wait_ge(got, u + 1)
                settle(pool)
                link = chain(pool, link_sem, 1, u)
                link(nc.gpsimd.tensor_scalar(rs[:, r, 0:1], mv[:, r, 1:2], EPS, None, ALU.add))
                nc.gpsimd.tensor_tensor(rs[:, r, 1:2], rs[:, r, 0:1], minus_half[:], ALU.pow).then_inc(done, 1)

            def max_parts(s, b):
                n = 2 * s.tile(0)[0] + b
                b = b % 2
                pool.wait_ge(S["max_ready"], HEADS * (n + 1))
                link = chain(pool, S["mpart_link"], 3, n)
                wait(pool, s, S["m_T"], n - 1)
                settle(pool)
                link(nc.gpsimd.tensor_copy(mpart[:, b, 0], mx[:, b]))
                link(nc.gpsimd.tensor_tensor(mrem[:, b], mx[:, b], mpart[:, b, 0], ALU.subtract))
                settle(pool)
                link(nc.gpsimd.tensor_copy(mpart[:, b, 1], mrem[:, b]))
                nc.gpsimd.tensor_tensor(mpart[:, b, 2], mrem[:, b], mpart[:, b, 1], ALU.subtract).then_inc(S["mpart_ready"], 1)

            def scatter_rows(s, choices):
                u, uh, r = s.tile(5)
                pool.wait_ge(S["route2"], u + 1)
                settle(pool)
                for k in choices:
                    nc.gpsimd.indirect_dma_start(out=xd, out_offset=IndexOnAxis(slots[:, r, k:k + 1], 0),
                                                 in_=pay[:, r], in_offset=None).then_inc(sc_out[r], 16)

            def body(s):
                if s.on(1):
                    max_parts(s, -1)
                if s.on(4):
                    u, uh, r = s.tile(4)
                    rstd(mv2, rs2, u, r, S["stats2"], S["rstd2_link"], S["rstd2"])
                if s.on(-2):
                    u, uh, r = s.tile(-2)
                    rstd(mv1, rs1, u, r, S["stats1"], S["rstd1_link"], S["rstd1"])
                    pool.wait_ge(S["k1_ready"], u + 1)
                    nc.gpsimd.tensor_tensor(kr[:], cs[:, r], parts[:, r, K1], ALU.subtract)
                if s.on(5):
                    scatter_rows(s, (0, 1))
                if s.on(-2):
                    u, uh, r = s.tile(-2)
                    pool.wait_ge(S["q1_ready"], u + 1)
                    nc.gpsimd.tensor_tensor(qf[:], qf[:], parts[:, r, Q1], ALU.subtract).then_inc(S["rem_ready"], 1)
                if s.on(0):
                    max_parts(s, 0)
                if s.on(3):
                    u, uh, r = s.tile(3)
                    pool.wait_ge(nat_in[r], 32 * (uh + 1))
                    pool.wait_ge(rdb_in, 16 * (u + 1))
                    link = chain(pool, S["x1_link"], 1, u)
                    link(nc.gpsimd.tensor_tensor(nat[:, r], nat[:, r], rdb[:], ALU.mult))
                    nc.gpsimd.tensor_tensor(xs[:, u], xs[:, u], nat[:, r], ALU.add).then_inc(S["x1_ready"], 1)
                if s.on(-2):
                    u, uh, r = s.tile(-2)
                    pool.wait_ge(S["k2q2_ready"], u + 1)
                    nc.gpsimd.tensor_tensor(parts[:, r, K3], kr[:], parts[:, r, K2], ALU.subtract)
                    nc.gpsimd.tensor_tensor(parts[:, r, Q3], qf[:], parts[:, r, Q2], ALU.subtract).then_inc(S["split_ready"], 1)
                if s.on(5):
                    scatter_rows(s, (2, 3))
            steps(pool, body)

            def scatter(quarter, r):
                i, iq, slot, on = etile(quarter, r, 2)
                if on:
                    pool.wait_ge(S["y_copied"], i + 1)
                    settle(pool)
                    nc.gpsimd.indirect_dma_start(out=yd, out_offset=IndexOnAxis(idxc[:, slot:slot + 1], 0),
                                                 in_=ysb[:, slot], in_offset=None, bounds_check=TOPK * TOK - 1,
                                                 oob_is_err=False).then_inc(y_out[slot], 16)
            chunk_loop(pool, scatter)

        @block.scalar
        def _(act_e):
            act_e.wait_ge(S["small_in"], 80)
            nc.scalar.activation(gates[:, 0:2], gates[:, 0:2], ACT.Tanh).then_inc(S["gates_ready"], 1)
            act_e.wait_ge(S["wr_T"], 1)
            nc.scalar.copy(wr[:], HB[:, 0:HC * E].rearrange("p (c e) -> p c e", c=HC)).then_inc(S["wr_ready"], 1)

            def body(s):
                for b in range(2):
                    for j in range(HEADS):
                        if s.on(1):
                            u = s.tile(1)[0]
                            n = PAIRS * u + HEADS * b + j
                            act_e.wait_ge(S["scores_T"], n + 1)
                            wait(act_e, s, S["pv_ready"], 2 * (2 * u + b - 1) + j // 4 + 1)
                            nc.scalar.activation(prob[:, j], ST[j % 2][:], ACT.Exp, scale=SCALE).then_inc(S["exp_ready"], 1)
                        at = HEADS * b + j
                        if s.on(-2):
                            u, uh, r = s.tile(-2)
                            if at == 3:
                                act_e.wait_ge(cs_in[r], 16 * (uh + 1))
                                wait(act_e, s, parts_out[r], 48 * uh)
                                wait(act_e, s, S["split_ready"], u)
                                nc.scalar.copy(parts[:, r, K1], cs[:, r]).then_inc(S["k1_ready"], 1)
                            if at == 6:
                                act_e.wait_ge(S["q_ready"], u + 1)
                                nc.scalar.copy(parts[:, r, Q1], qf[:]).then_inc(S["q1_ready"], 1)
                            if at == 9:
                                act_e.wait_ge(S["rem_ready"], u + 1)
                                nc.scalar.copy(parts[:, r, K2], kr[:])
                            if at == 10:
                                nc.scalar.copy(parts[:, r, Q2], qf[:]).then_inc(S["k2q2_ready"], 1)
                        if at == 2 and s.on(0):
                            t, th, r = s.tile(0)
                            act_e.wait_ge(S["v_T"], t + 1)
                            wait(act_e, s, S["pv_ready"], 4 * (t - 1))
                            nc.scalar.copy(vt[:, r, :, :, 0:DH],
                                           HB[:, 0:2 * P].rearrange("p (c j v) -> p c j v", c=2, j=PAIRS)).then_inc(S["v_T_copied"], 1)
                        if j == 3 and (s.on(0) if b else s.on(1)):
                            n = 2 * s.tile(0)[0] + b - 1
                            rm = (b - 1) % 2
                            slot = (2 * s.odd + b - 1) % 4
                            act_e.wait_ge(S["m_T"], n + 1)
                            wait(act_e, s, mrow_in[(slot - 2) % 4], 16 * ((s.half if 2 * s.odd + b - 1 >= 0 else s.half - 1) + (1 if slot >= 2 else 0)))
                            nc.scalar.copy(mT[:, rm], MVB[0:MB_PARTS * PAIRS, 0:P // 2].bitcast(BF16)).then_inc(S["m_T_copied"], 1)
                        if j == 4 and (s.on(1) if b else s.on(2)):
                            n = 2 * s.tile(0)[0] + b - 3
                            act_e.wait_ge(S["pv_ready"], 2 * (n + 1))
                            wait(act_e, s, o_out, 16 * n)
                            nc.scalar.copy(osb[:], PV[:]).then_inc(S["o_copied"], 1)
                        if at == 8 and s.on(4):
                            u = s.tile(4)[0]
                            act_e.wait_ge(S["h_T"], u + 1)
                            wait(act_e, s, S["logits"], u)
                            nc.scalar.copy(hT[:], HB[:, 2 * P:4 * P].rearrange("p (c q) -> p c q", c=HC)).then_inc(S["h_T_copied"], 1)
            steps(act_e, body)

            act_e.wait_ge(S["wts_link"], 1)
            nc.scalar.activation(wts[:], wts[:], ACT.Exp).then_inc(S["exp_w"], 1)

            def expert_act(quarter, r):
                i, iq, slot, on = etile(quarter, r, 1)
                if on:
                    act_e.wait_ge(S["act_T"], i + 1)
                    if not isinstance(i, int) or i >= 2:
                        act_e.wait_ge(S["y_ready"], i - 1)
                    nc.scalar.copy(actT[:, slot % 2], ATB[:, 0:D]).then_inc(S["act_T_copied"], 1)
                i, iq, slot, on = etile(quarter, r, -1)
                if on:
                    act_e.wait_ge(S["x_T"], i + 1)
                    if not isinstance(i, int) or i >= 2:
                        act_e.wait_ge(S["gu_ready"], i - 1)
                    nc.scalar.copy(xT[:, slot % 2], XTB[:, 0:H]).then_inc(S["x_T_copied"], 1)
                i, iq, slot, on = etile(quarter, r, 0)
                if on:
                    act_e.wait_ge(S["gate_ready"], i + 1)
                    if not isinstance(i, int) or i >= 2:
                        act_e.wait_ge(S["act_ready"], i - 1)
                    nc.scalar.activation(glu[:, slot % 2], gub[:, slot % 2, :, 0], ACT.Sigmoid, scale=ALPHA).then_inc(S["sig_ready"], 1)
            chunk_loop(act_e, expert_act)

        @block.vector
        def _(dve):
            nc.vector.memset(PV[:], 0.0)
            dve.wait_ge(S["consts"], 1)
            dve.wait_ge(S["gates_ready"], 1)
            nc.vector.tensor_tensor(gates[:, 2:3], gates[:, 0:1], gates[:, 2:3], ALU.mult).then_inc(S["gates_ready"], 1)
            dve.wait_ge(S["gates_ready"], 2)

            def route(s, at):
                u, uh, r = s.tile(4)
                if s.on(4):
                    done = 10 * u
                    if at == 10:
                        dve.wait_ge(S["logits"], u + 1)
                        nc.vector.tensor_tensor(lg[:], RB[:, 0:E], br[:], ALU.add).then_inc(S["route_link"], 1)
                    if at == 11:
                        dve.wait_ge(S["route_link"], done + 1)
                        settle(dve)
                        nc.vector.max(best[:], lg[:]).then_inc(S["route_link"], 1)
                    if at == 12:
                        dve.wait_ge(S["route_link"], done + 2)
                        nc.vector.tensor_copy(top[:, bass.ds(u, 1)], best[:].unsqueeze(1))
                        nc.vector.max_index(tidx[:], best[:], lg[:]).then_inc(S["route_link"], 1)
                        dve.wait_ge(S["route_link"], done + 3)
                        nc.vector.tensor_copy(tidf[:], tidx[:, 0:TOPK]).then_inc(S["route_link"], 1)
                    if at == 13:
                        dve.wait_ge(S["route_link"], done + 4)
                        nc.vector.tensor_tensor(hot[:], e_iota, tidf[:].unsqueeze(2).to_broadcast([P, TOPK, E]),
                                                ALU.is_equal).then_inc(S["route_link"], 1)
                    if at == 14:
                        dve.wait_ge(S["route_link"], done + 5)
                        with nc.allow_low_precision("counts up to 16"):
                            nc.vector.tensor_reduce(pick[:, r], hot[:].rearrange("p k e -> p e k"), AX.X, ALU.add).then_inc(S["route_link"], 1)
                        nc.vector.tensor_tensor(tmp[:], hot[:], k_base, ALU.mult).then_inc(S["route_link"], 1)
                    if at == 15:
                        dve.wait_ge(S["route_link"], done + 7)
                        nc.vector.tensor_tensor(seen[:, 1 - r], seen[:, r], pick[:, r], ALU.add).then_inc(S["route1"], 1)
                        nc.vector.tensor_reduce(dst[:], tmp[:].rearrange("p k e -> p e k"), AX.X, ALU.add).then_inc(S["route_link"], 1)
                u, uh, r = s.tile(5)
                if s.on(5):
                    done = 10 * u + 8
                    if at == 0:
                        dve.wait_ge(S["route_link"], done)
                        settle(dve)
                        nc.vector.tensor_scalar(pay[:, r, H:PW].bitcast(U32), dst[:], tok_f[:, bass.ds(u, 1)], None, ALU.add)
                    if at == 2:
                        dve.wait_ge(S["ranks"], u + 1)
                        nc.vector.tensor_tensor(slot_base[:], RB[:, E:2 * E], e_region, ALU.add).then_inc(S["route_link"], 1)
                    if at == 3:
                        dve.wait_ge(S["route_link"], done + 1)
                        nc.vector.tensor_tensor(tmp[:], hot[:], slot_base[:].unsqueeze(1).to_broadcast([P, TOPK, E]),
                                                ALU.mult).then_inc(S["route_link"], 1)
                    if at == 4:
                        dve.wait_ge(S["route_link"], done + 2)
                        with nc.allow_low_precision("whole numbers under 2 ** 24"):
                            nc.vector.tensor_reduce(slots[:, r], tmp[:], AX.X, ALU.add).then_inc(S["route2"], 1)

            def body(s):
                for at in range(PAIRS):
                    b, j = divmod(at, HEADS)
                    if s.on(0):
                        t = s.tile(0)[0]
                        dve.wait_ge(S["scores"], PAIRS * t + at + 1)
                        if j == 0:
                            wait(dve, s, S["mpart_ready"], 2 * t + b - 1)
                        nc.vector.tensor_reduce(mx[:, b, 2 * j:2 * j + 2], S1[j % 2][:].rearrange("p (c l) -> p c l", c=2),
                                                AX.X, ALU.max).then_inc(S["max_ready"], 1)
                    if s.on(4) and at == 0:
                        u, uh, r = s.tile(4)
                        dve.wait_ge(S["x1_ready"], u + 1)
                        nc.vector.bn_stats(st2[:], xs[:, u]).then_inc(S["stats2_link"], 1)
                    if s.on(4) and at == 1:
                        u, uh, r = s.tile(4)
                        dve.wait_ge(S["stats2_link"], u + 1)
                        settle(dve)
                        nc.vector.bn_aggr(mv2[:, r], st2[:]).then_inc(S["stats2"], 1)
                    if s.on(-2) and at == 1:
                        u, uh, r = s.tile(-2)
                        if not s.loop and u == 0:
                            dve.wait_ge(S["x_in"], 16)
                        else:
                            dve.wait_ge(S["x_in"], 16 * NT)
                        nc.vector.bn_stats(st1[:], xs[:, u]).then_inc(S["stats1_link"], 1)
                    if s.on(-2) and at == 2:
                        u, uh, r = s.tile(-2)
                        dve.wait_ge(S["stats1_link"], u + 1)
                        settle(dve)
                        nc.vector.bn_aggr(mv1[:, r], st1[:]).then_inc(S["stats1"], 1)
                    if s.on(4) and at == 4:
                        u, uh, r = s.tile(4)
                        dve.wait_ge(S["rstd2"], u + 1)
                        wait(dve, s, sc_out[r], 16 * TOPK * uh)
                        nc.vector.tensor_scalar(pay[:, r, 0:H], xs[:, u], mv2[:, r, 0:1], rs2[:, r, 1:2],
                                                ALU.subtract, ALU.mult).then_inc(S["h_ready"], 1)
                    if s.on(-2) and at == 5:
                        u, uh, r = s.tile(-2)
                        dve.wait_ge(S["rstd1"], u + 1)
                        wait(dve, s, S["split_ready"], u)
                        nc.vector.tensor_scalar(qf[:], xs[:, u], mv1[:, r, 0:1], rs1[:, r, 1:2],
                                                ALU.subtract, ALU.mult).then_inc(S["q_ready"], 1)
                    if s.on(2) and at == 13:
                        u, uh, r = s.tile(2)
                        dve.wait_ge(nat_in[r], 32 * (uh + 1))
                        wait(dve, s, S["rd_out"], 16 * (u - 1))
                        nc.vector.reciprocal(rden[:, r], den[:, r]).then_inc(S["pow_link"], 1)
                    if s.on(2) and at == 14:
                        u, uh, r = s.tile(2)
                        dve.wait_ge(S["pow_link"], u + 1)
                        nc.vector.tensor_scalar(rden[:, r], rden[:, r], gates[:, 2:3], None, ALU.mult).then_inc(S["rden_ready"], 1)
                    route(s, at)
            steps(dve, body)

            link = chain(dve, S["table_link"], 20, 0)
            dve.wait_ge(S["counts"], 1)
            link(nc.vector.tensor_copy(cnt[:, 0], RB[0:1, 0:E]))
            link(nc.vector.tensor_scalar(cnti[:, 0], cnt[:, 0], float(P - 1), None, ALU.add))
            link(nc.vector.tensor_scalar(cnti[:, 1], cnti[:, 0], 7, None, ALU.arith_shift_right))
            link(nc.vector.tensor_copy(cnt[:, 1], cnti[:, 1]))
            link(nc.vector.tensor_copy(cnt[:, 2:6], cnt[:, 1:2].to_broadcast([1, 4, E])))
            src = 1
            for n, by in enumerate((1, 2, 4, 8)):
                link(nc.vector.tensor_copy(cnt[:, 2 + n, 0:by], cnt[:, src, 0:by]))
                link(nc.vector.tensor_tensor(cnt[:, 2 + n, by:E], cnt[:, src, by:E], cnt[:, src, 0:E - by], ALU.add))
                src = 2 + n
            ends = cnt[:, src]
            nc.vector.tensor_tensor(padrow[:], cnt[:, 0], e_region[0:1], ALU.add)
            link(nc.vector.tensor_tensor(cmp[:], ends.unsqueeze(1).to_broadcast([1, MT, E]),
                                         tile_f[:].unsqueeze(2).to_broadcast([1, MT, E]), ALU.is_le))
            link(nc.vector.tensor_tensor(cmpn[:], cmp[:], cnt[:, 1].unsqueeze(1).to_broadcast([1, MT, E]), ALU.mult))
            nc.vector.tensor_reduce(tabf[:, 0], cmp[:], AX.X, ALU.add)
            link(nc.vector.tensor_reduce(tabf[:, 1], cmpn[:], AX.X, ALU.add))
            nc.vector.tensor_scalar(tabf[:, 2], tabf[:, 0], float(E), float(P), ALU.is_lt, ALU.mult)
            link(nc.vector.tensor_tensor(tabf[:, 3], tile_f[:], tabf[:, 1], ALU.subtract))
            link(nc.vector.tensor_tensor(tabf[:, 4], tabf[:, 3], tabf[:, 2], ALU.mult))
            link(nc.vector.scalar_tensor_tensor(tab[:, 0], tabf[:, 0], float(REGION), tabf[:, 4], ALU.mult, ALU.add))
            nc.vector.tensor_scalar(tab[:, 1], tabf[:, 0], float(E - 1), None, ALU.min).then_inc(S["table_ready"], 1)
            wlink = chain(dve, S["wts_link"], 4, 0)
            wlink(nc.vector.tensor_tensor(wts[:], top[:, :, 0:TOPK], top[:, :, 0:1].to_broadcast([P, NT, TOPK]), ALU.subtract))
            dve.wait_ge(S["exp_w"], 1)
            wlink(nc.vector.tensor_reduce(wsum[:], wts[:], AX.X, ALU.add))
            wlink(nc.vector.reciprocal(wsum[:], wsum[:]))
            wlink(nc.vector.tensor_scalar(wsum[:], wsum[:], gates[:, 1:2], None, ALU.mult))
            nc.vector.tensor_tensor(wts[:], wts[:], wsum[:].unsqueeze(2).to_broadcast([P, NT, TOPK]), ALU.mult).then_inc(S["wts_ready"], 1)
            dve.wait_ge(S["table_ready"], 1)
            dve.wait_ge(S["bias_in"], 32)

            experts = {}

            def expert_dve(quarter, r):
                i, iq, slot, on = etile(quarter, r, 0)
                gate, up = gub[:, slot % 2, :, 0], gub[:, slot % 2, :, 1]
                if on:
                    e = dve.value_load(tab[0:1, 1, bass.ds(i, 1)], min_val=0, max_val=E - 1)
                    dve.wait_ge(xt_in[slot], 16 * (iq + 1))
                    if not isinstance(i, int) or i >= 4:
                        dve.wait_ge(y_out[slot], 16 * iq)
                    nc.vector.tensor_copy(idxc[:, slot:slot + 1], xt[:, slot, bass.ds(e + H, 1)].bitcast(U32)).then_inc(S["dest_ready"], 1)
                    dve.wait_ge(S["gu_ready"], i + 1)
                    link = chain(dve, S["act_link"], 2, i)
                    link(nc.vector.tensor_tensor(gub[:, slot % 2].rearrange("p f two -> p (f two)"), GU[slot % 2][:],
                                                 bias_gu[:, e], ALU.add))
                    nc.vector.tensor_scalar(gate, gate, LIMIT, None, ALU.min).then_inc(S["gate_ready"], 1)
                    nc.vector.tensor_scalar(up, up, LIMIT, -LIMIT, ALU.min, ALU.max)
                j, jq, jslot, jon = etile(quarter, r, 2)
                if jon:
                    ej = dve.value_load(tab[0:1, 1, bass.ds(j, 1)], min_val=0, max_val=E - 1)
                    dve.wait_ge(S["y_ready"], j + 1)
                    if not isinstance(j, int) or j >= 4:
                        dve.wait_ge(y_out[jslot], 16 * jq)
                    nc.vector.tensor_tensor(ysb[:, jslot], YB[jslot % 2][:, 0:H], bias_dn[:, ej], ALU.add).then_inc(S["y_copied"], 1)
                if on:
                    dve.wait_ge(S["sig_ready"], i + 1)
                    link(nc.vector.tensor_tensor(glu[:, slot % 2], gate, glu[:, slot % 2], ALU.mult))
                    if not isinstance(i, int) or i >= 2:
                        dve.wait_ge(S["act_T"], i - 1)
                    nc.vector.scalar_tensor_tensor(act[:, slot % 2], up, 1.0, glu[:, slot % 2], ALU.add, ALU.mult).then_inc(S["act_ready"], 1)
            chunk_loop(dve, expert_dve)

            for u in range(NT):
                dve.wait_ge(yk_in[u % 2], 16 * (u // 2 + 1))
                if u >= 2:
                    dve.wait_ge(fin_out[u % 2], 16 * (u // 2))
                link = chain(dve, S["sum_link"], TOPK - 1, u)
                for k in range(TOPK):
                    acc = xs[:, u] if k == 0 else fin[:, u % 2]
                    ins = nc.vector.scalar_tensor_tensor(fin[:, u % 2], yk[:, u % 2, k], wts[:, u, k:k + 1], acc, ALU.mult, ALU.add)
                    if k < TOPK - 1:
                        link(ins)
                    else:
                        ins.then_inc(S["fin_ready"], 1)

        @block.tensor
        def _(pe):
            pe.wait_ge(S["consts"], 1)
            pe.wait_ge(S["small_in"], 80)
            for c in range(HC):
                ins = nc.tensor.transpose(HB[:, c * E:(c + 1) * E], wr_nat[:, c * P:(c + 1) * P], ident[0:E, 0:E])
            ins.then_inc(S["wr_T"], 1)
            pe.wait_ge(S["wr_ready"], 1)

            def value_product(s, n, lag, b, quad):
                u, uh, r = s.tile(lag)
                pe.wait_ge(S["exp_ready"], HEADS * n + 4 * quad + 4)
                if quad == 0:
                    wait(pe, s, S["o_copied"], n)
                    pe.wait_ge(S["v_T_copied"], u + 1)
                for c in range(2):
                    for jj in range(4):
                        j = 4 * quad + jj
                        ins = nc.tensor.matmul(PV[32 * jj:32 * jj + 2 * DH, quad * L:(quad + 1) * L],
                                               vt[:, r, c, HEADS * b + j], prob[:, j, c * L:(c + 1) * L],
                                               start=(c == 0), stop=(c == 1))
                ins.then_inc(S["pv_ready"], 1)

            def body(s):
                if s.on(5):
                    u, uh, r = s.tile(5)
                    pe.wait_ge(S["route1"], u + 1)
                    nc.tensor.matmul(RB[:, E:2 * E], before[:], pick[:, r], start=True, stop=False)
                    nc.tensor.matmul(RB[:, E:2 * E], ones[:], seen[:, r], start=False, stop=True).then_inc(S["ranks"], 1)
                if s.on(0):
                    t, th, r = s.tile(0)
                    pe.wait_ge(cv_in[r], 16 * (th + 1))
                    wait(pe, s, S["v_T_copied"], t)
                    for c in range(2):
                        ins = nc.tensor.transpose(HB[:, c * P:(c + 1) * P], cv[:, r, c * P:(c + 1) * P], ident[:])
                    ins.then_inc(S["v_T"], 1)
                t = s.tile(0)[0]
                for at in range(PAIRS):
                    b, j = divmod(at, HEADS)
                    if s.on(1):
                        u, uh, r = s.tile(1)
                        slot = 2 * r + b
                        n = PAIRS * u + at
                        if j == 0:
                            pe.wait_ge(mrow_in[slot], 16 * (uh + 1))
                        wait(pe, s, S["exp_ready"], n - 1)
                        for c in range(2):
                            ins = nc.tensor.matmul(ST[j % 2][:, c * L:(c + 1) * L],
                                                   stk[0:MROW + MB_PARTS, slot, 1, j, c * P:(c + 1) * P],
                                                   stk[0:MROW + MB_PARTS, slot, 0, j], start=True, stop=True)
                        ins.then_inc(S["scores_T"], 1)
                    if s.on(0):
                        t, th, r = s.tile(0)
                        slot = 2 * r + b
                        if j == 0:
                            pe.wait_ge(stk_in[slot], 16 * (th + 1))
                        wait(pe, s, S["max_ready"], PAIRS * t + at - 1)
                        for c in range(2):
                            ins = nc.tensor.matmul(S1[j % 2][:, c * L:(c + 1) * L],
                                                   stk[0:MROW, slot, 0, j, c * P:(c + 1) * P],
                                                   stk[0:MROW, slot, 1, j], start=True, stop=True)
                        ins.then_inc(S["scores"], 1)
                    if j == 2 and (s.on(0) if b else s.on(1)):
                        n = 2 * t + b - 1
                        pe.wait_ge(S["mpart_ready"], n + 1)
                        wait(pe, s, S["m_T_copied"], n)
                        settle(pe)
                        nc.tensor.transpose(MVB[0:MB_PARTS * PAIRS, 0:P // 2].bitcast(BF16),
                                            mpart[:, (b - 1) % 2].rearrange("p s j -> p (s j)"),
                                            identb[:]).then_inc(S["m_T"], 1)
                    if at == 6 and s.on(4):
                        u, uh, r = s.tile(4)
                        pe.wait_ge(S["h_ready"], u + 1)
                        wait(pe, s, S["h_T_copied"], u)
                        for c in range(HC):
                            ins = nc.tensor.transpose(HB[:, (2 + c) * P:(3 + c) * P], pay[:, r, c * P:(c + 1) * P], ident[:])
                        ins.then_inc(S["h_T"], 1)
                    if at == 9 and s.on(4):
                        u = s.tile(4)[0]
                        pe.wait_ge(S["h_T_copied"], u + 1)
                        wait(pe, s, S["route1"], u)
                        for c in range(HC):
                            ins = nc.tensor.matmul(RB[:, 0:E], hT[:, c], wr[:, c], start=(c == 0), stop=(c == HC - 1))
                        ins.then_inc(S["logits"], 1)
                    if j == 3:
                        lag = 1 if b else 2
                        if s.on(lag):
                            value_product(s, 2 * t + b - 3, lag, (b - 3) % 2, 1)
                    if j == 7 and s.on(1):
                        value_product(s, 2 * t + b - 2, 1, b, 0)
            steps(pe, body)

            pe.wait_ge(S["route2"], NT)
            nc.tensor.matmul(RB[:, 0:E], ones[:], seen[:, NT % 2], start=True, stop=True).then_inc(S["counts"], 1)
            pe.wait_ge(S["table_ready"], 1)
            pe.wait_ge(S["w_in"], 32 * E)

            def expert_pe(quarter, r):
                i, iq, slot, on = etile(quarter, r, 0)
                if on:
                    e = pe.value_load(tab[0:1, 1, bass.ds(i, 1)], min_val=0, max_val=E - 1)
                    pe.wait_ge(S["x_T_copied"], i + 1)
                    if not isinstance(i, int) or i >= 2:
                        pe.wait_ge(S["gate_ready"], i - 1)
                    for c in range(HC):
                        ins = nc.tensor.matmul(GU[slot % 2][:], xT[:, slot % 2, c * P:(c + 1) * P], wgu[:, e, c],
                                               start=(c == 0), stop=(c == HC - 1))
                    ins.then_inc(S["gu_ready"], 1)
                i, iq, slot, on = etile(quarter, r, 1)
                if on:
                    pe.wait_ge(S["act_ready"], i + 1)
                    if not isinstance(i, int) or i >= 1:
                        pe.wait_ge(S["act_T_copied"], i)
                    for c in range(HC):
                        ins = nc.tensor.transpose(ATB[:, c * P:(c + 1) * P], act[:, slot % 2, c * P:(c + 1) * P], ident[:])
                    ins.then_inc(S["act_T"], 1)
                i, iq, slot, on = etile(quarter, r, -1)
                if on:
                    pe.wait_ge(xt_in[slot], 16 * (iq + 1))
                    if not isinstance(i, int) or i >= 1:
                        pe.wait_ge(S["x_T_copied"], i)
                    for c in range(HC):
                        ins = nc.tensor.transpose(XTB[:, c * P:(c + 1) * P], xt[:, slot, c * P:(c + 1) * P], ident[:])
                    ins.then_inc(S["x_T"], 1)
                i, iq, slot, on = etile(quarter, r, 2)
                if on:
                    e = pe.value_load(tab[0:1, 1, bass.ds(i, 1)], min_val=0, max_val=E - 1)
                    pe.wait_ge(S["act_T_copied"], i + 1)
                    if not isinstance(i, int) or i >= 2:
                        pe.wait_ge(S["y_copied"], i - 1)
                    for c in range(HC):
                        ins = nc.tensor.matmul(YB[slot % 2][:, 0:H], actT[:, slot % 2, c * P:(c + 1) * P], wdn[:, e, c],
                                               start=(c == 0), stop=(c == HC - 1))
                    ins.then_inc(S["y_ready"], 1)
            chunk_loop(pe, expert_pe)


_INS = ["x", "ctx_2048", "g_xattn", "g_ffn", "L0_xattn_gamma", "L0_ffn_router_weight", "L0_ffn_router_bias",
        "L0_ffn_gate_up_proj", "L0_ffn_gate_up_proj_bias", "L0_ffn_down_proj", "L0_ffn_down_proj_bias"]


def kernel(**inputs):
    import numpy as np
    import concourse.bacc as bacc
    from concourse.bass_utils import run_bass_kernel_spmd

    nc = bacc.Bacc("TRN2", target_bir_lowering=False, num_devices=1)
    arrays, args = {}, []
    for name in _INS:
        a = np.ascontiguousarray(inputs[name])
        if a.ndim == 0:
            a = a.reshape(1, 1)
        arrays[f"in_{name}"] = a
        args.append(nc.dram_tensor(f"in_{name}", a.shape, mybir.dt.from_np(a.dtype), kind="ExternalInput").ap())
    out = nc.dram_tensor("out_x", inputs["x"].shape, F32, kind="ExternalOutput").ap()
    flamingo_gated_kernel(nc, *args, out)
    r = run_bass_kernel_spmd(nc, [arrays], core_ids=[0])
    return r.results[0]["out_x"]
```

```python
from contextlib import ExitStack

import concourse.bass as bass
from concourse import mybir

F32 = mybir.dt.float32
BF16 = mybir.dt.bfloat16
U32 = mybir.dt.uint32
I32 = mybir.dt.int32
ALU = mybir.AluOpType
ACT = mybir.ActivationFunctionType
AX = mybir.AxisListType
IndexOnAxis = bass.IndirectOffsetOnAxis

P = 128
EPS = 1e-5
ALPHA = 1.702
LIMIT = 7.0
HEADS = 8
TOPK = 4
MROW = 96
MB_PARTS = 3


def flamingo_gated_kernel(nc, x, ctx_in, g_xattn, g_ffn, gamma, router_w, router_b,
                          gate_up, gate_up_b, down, down_b, out):
    NB, CH, L = x.shape
    DH = CH // HEADS
    E, H, F2 = gate_up.shape
    D = F2 // 2
    TOK = NB * CH
    NT = TOK // P
    PAIRS = 2 * HEADS
    HC = H // P
    SCALE = float(DH) ** -0.5
    NPROD = 6
    STK = NPROD * DH
    REGION = P + TOK
    ROWS = E * REGION + P
    YSLOTS = 12
    PW = H + E
    MT = (TOK * TOPK - E) // P + E
    MWORDS = (MT + 5) // 4
    SKIP = 2 * TOK * TOPK
    assert (P, L) == (2 * CH, H)

    x_rows = x.rearrange("b c l -> (b c) l")
    ctx_rows = ctx_in.rearrange("b c l -> (b c) l")
    out_rows = out.rearrange("b c l -> (b c) l")

    stacks = nc.dram_tensor("stacks", [NT, 2 * NPROD, P, L], BF16, kind="Internal").ap()
    att_raw = nc.dram_tensor("att_raw", [NB * 2, P, L], F32, kind="Internal").ap()
    rden_dram = nc.dram_tensor("rden_dram", [NB * HEADS, L], F32, kind="Internal").ap()
    xd = nc.dram_tensor("xd", [ROWS, PW], F32, kind="Internal").ap()
    yd = nc.dram_tensor("yd", [TOPK * TOK, H], F32, kind="Internal").ap()

    with ExitStack() as stack:
        def sb(name, shape, dt):
            return stack.enter_context(nc.sbuf_tensor(name, shape, dt))

        def sem(name):
            return stack.enter_context(nc.semaphore(name))

        bank = [stack.enter_context(nc.psum_tensor(f"bank{i}", [P, 512], F32)) for i in range(8)]
        S1, ST = bank[0:2], bank[2:4]
        PV, MVB, HB, RB = bank[4:8]
        GU, XTB, ATB, YB = bank[0:2], bank[2], bank[3], bank[4:6]

        wgu = sb("wgu", [P, E, HC, F2], F32)
        wdn = sb("wdn", [P, E, HC, H], F32)
        xs = sb("xs", [P, NT, L], F32)
        area = sb("area", [P, 3 * 4096], F32)
        cs = area[:, 0:512].rearrange("p (s l) -> p s l", s=2)
        cv = area[:, 512:1024].rearrange("p (s l) -> p s l", s=2)
        stk = area[:, 4096:12288].bitcast(BF16).rearrange("p (s two j l) -> p s two j l", s=4, two=2, j=HEADS)
        bias_dn = area[:, 0:E * H].rearrange("p (e f) -> p e f", e=E)
        bias_gu = area[:, E * H:E * H + E * F2].rearrange("p (e f) -> p e f", e=E)
        work = sb("work", [P, 7680], F32)
        prob = work[:, 0:4096].rearrange("p (s l) -> p s l", s=HEADS)
        vt = work[:, 4096:5120].rearrange("p (s c j v) -> p s c j v", s=2, c=2, j=PAIRS)
        osb = work[:, 5120:5632]
        qf = work[:, 5632:5888]
        kr = work[:, 5888:6144]
        parts = work[:, 6144:7680].bitcast(BF16).rearrange("p (s n l) -> p s n l", s=2, n=2 * MB_PARTS)
        Q3, Q2, Q1, K1, K2, K3 = range(6)
        xt = work[:, 0:4 * PW].rearrange("p (s f) -> p s f", s=4)
        o = 4 * PW
        ysb = work[:, o:o + 4 * H].rearrange("p (s f) -> p s f", s=4)
        o += 4 * H
        xT = work[:, o:o + 2 * H].rearrange("p (s f) -> p s f", s=2)
        o += 2 * H
        actT = work[:, o:o + 2 * D].rearrange("p (s f) -> p s f", s=2)
        o += 2 * D
        gub = work[:, o:o + 2 * F2].rearrange("p (s f two) -> p s f two", s=2, two=2)
        o += 2 * F2
        glu = work[:, o:o + 2 * D].rearrange("p (s f) -> p s f", s=2)
        o += 2 * D
        act = work[:, o:o + 2 * D].rearrange("p (s f) -> p s f", s=2)
        assert o + 2 * D <= 7680
        yk = area[:].rearrange("p (s k f) -> p s k f", s=YSLOTS, k=TOPK)

        st1 = sb("st1", [P, 6], F32)
        mv1 = sb("mv1", [P, 2, 2], F32)
        rs1 = sb("rs1", [P, 2, 2], F32)
        st2 = sb("st2", [P, 6], F32)
        mv2 = sb("mv2", [P, 2, 2], F32)
        rs2 = sb("rs2", [P, 2, 2], F32)
        mx = sb("mx", [P, 2, PAIRS], F32)
        mrem = sb("mrem", [P, 2, PAIRS], F32)
        mpart = sb("mpart", [P, 2, MB_PARTS, PAIRS], BF16)
        mT = sb("mT", [MB_PARTS * PAIRS, 2, P], BF16)
        nat = sb("nat", [P, 2, L], F32)
        den = sb("den", [P, 2, 32], F32)
        rden = sb("rden", [P, 2, 32], F32)
        rdb = sb("rdb", [P, L], F32)
        pay = sb("pay", [P, 2, PW], F32)
        hT = sb("hT", [P, HC, P], F32)
        zpay = sb("zpay", [P, PW], F32)
        wr = sb("wr", [P, HC, E], F32)
        wr_nat = sb("wr_nat", [E, H], F32)
        br = sb("br", [P, E], F32)
        lg = sb("lg", [P, E], F32)
        top = sb("top", [P, NT, 8], F32)
        best = sb("best", [P, 8], F32)
        tidx = sb("tidx", [P, 8], U32)
        hot = sb("hot", [P, TOPK, E], F32)
        tmp = sb("tmp", [P, TOPK, E], F32)
        dst = sb("dst", [P, E], F32)
        pick = sb("pick", [P, 2, E], BF16)
        seen = sb("seen", [P, 2, E], BF16)
        slot_base = sb("slot_base", [P, E], F32)
        slots = sb("slots", [P, 2, TOPK], U32)
        wts = sb("wts", [P, NT, TOPK], F32)
        wsum = sb("wsum", [P, NT], F32)
        gates = sb("gates", [P, 3], F32)
        minus_half = sb("minus_half", [P, 1], F32)
        ident = sb("ident", [P, P], F32)
        identb = sb("identb", [P, P], BF16)
        before = sb("before", [P, P], BF16)
        ones = sb("ones", [P, P], BF16)
        iota_i = work[:, 0:3 * TOPK * E].bitcast(I32).rearrange("p (n k e) -> p n k e", n=3, k=TOPK)
        iota_f = sb("iota_f", [P, 3, TOPK, E], F32)
        e_iota, k_base, e_region = iota_f[:, 0], iota_f[:, 1], iota_f[:, 2, 0]
        tok_i = sb("tok_i", [P, NT], I32)
        tok_f = sb("tok_f", [P, NT], F32)
        upto = sb("upto", [P, E, E], F32)
        minus_row = sb("minus_row", [P, 1], F32)
        tile_no = sb("tile_no", [P, 1], F32)
        cnt, tiles_of, ends, begins, base, started, done, held = (sb(n, [P, E], F32) for n in
            ("cnt", "tiles_of", "ends", "begins", "base", "started", "done", "held"))
        cnti = sb("cnti", [P, 2, E], I32)
        sums = work[:, 4096:4096 + E * E].rearrange("p (a e) -> p a e", a=E)
        ntab = sb("ntab", [P, 4], F32)
        etab = sb("etab", [1, 4 * MWORDS + 2], F32)
        word = sb("word", [1, MWORDS], F32)
        tab_row = sb("tab_row", [1, MT], I32)
        tab_word = sb("tab_word", [1, MWORDS], I32)
        idxc = sb("idxc", [P, 4], U32)

        names = """passed x_in small_in w_in bias_in consts gates_ready wr_T wr_ready
            stats1 var1 var2 rstd1 q_ready k1_ready q1_ready kr_ready rem_ready k2_ready q2_ready split_ready stats1_link
            scores scores_T max_ready exp_ready pv_ready mpart_ready mpart_link m_T m_T_copied
            v_T v_T_copied o_copied rden_ready x1_ready x1_link stats2 stats2_link rstd2 h_ready h_T
            h_T_copied logits route_link route1 ranks route2 scattered counts table_link tile_rows_ready tile_rows_T table_ready stacks_set half_set zpay_set late_link late_consts
            x_T x_T_copied gu_ready act_T act_T_copied y_ready y_copied biased gate_ready sig_ready act_link
            act_ready dest_ready wts_link wts_ready exp_w fin_ready rd_out zero_in x_in_next x_in_late setup_link sum_link pow_link""".split()
        S = {n: sem(n) for n in names}
        parts_out = [sem(f"parts_out{i}") for i in range(2)]
        stk_in = [sem(f"stk_in{i}") for i in range(4)]
        mrow_in = [sem(f"mrow_in{i}") for i in range(4)]
        cs_in = [sem(f"cs_in{i}") for i in range(2)]
        cv_in = [sem(f"cv_in{i}") for i in range(2)]
        o_out = sem("o_out")
        nat_in = [sem(f"nat_in{i}") for i in range(2)]
        rdb_in = sem("rdb_in")
        sc_out = [sem(f"sc_out{i}") for i in range(2)]
        xt_in = [sem(f"xt_in{i}") for i in range(4)]
        y_out = [sem(f"y_out{i}") for i in range(4)]
        yk_in = [sem(f"yk_in{i}") for i in range(YSLOTS)]
        fin_out = sem("fin_out")

        class Step:
            def __init__(self, half, odd):
                self.half, self.odd, self.loop = half, odd, not isinstance(half, int)

            def on(self, lag):
                return self.loop or 0 <= 2 * self.half + self.odd - lag < NT

            def tile(self, lag):
                a, odd = divmod(self.odd - lag, 2)
                return 2 * self.half + 2 * a + odd, self.half + a, odd

            def least(self, v, small):
                return self.loop or v >= small

        LAST = NT + 5
        WARM = 11

        def steps(eng, body):
            for t in range(-2, 6):
                body(Step(t // 2, t % 2))
            with eng.Fori(3, 7) as half:
                body(Step(half, 0))
                body(Step(half, 1))
            for t in range(14, LAST):
                body(Step(t // 2, t % 2))

        def wait(eng, step, s, v):
            if step.least(v, 1):
                eng.wait_ge(s, v)

        def settle(eng):
            eng.sem_inc(S["passed"], 1)

        def chain(eng, s, per, u):
            count = [0]

            def link(ins):
                count[0] += 1
                assert count[0] <= per
                ins.then_inc(s, 1)
                eng.wait_ge(s, u * per + count[0])
            return link

        def chunk_loop(eng, body):
            for i in range(-1, 8):
                body(i // 4, i % 4)
            last = (MT - 1) // 4
            with eng.Fori(2, last) as quarter:
                for r in range(4):
                    body(quarter, r)
            for i in range(4 * last, MT + 2):
                body(i // 4, i % 4)

        def etile(quarter, r, lag):
            a, slot = divmod(r - lag, 4)
            i = 4 * quarter + 4 * a + slot
            return i, quarter + a, slot, (not isinstance(i, int)) or 0 <= i < MT

        def tile_rows(rows, u):
            return rows[bass.ds(P * u, P)].rearrange("(a d) l -> d a l", d=DH)

        def experts_of(eng, quarter):
            held_word = eng.value_load(tab_word[0:1, bass.ds(quarter, 1)], min_val=0, max_val=2 ** 24 - 1)
            return lambda k: (held_word >> (4 * (k + 2))) & (E - 1)

        block = stack.enter_context(nc.Block())

        @block.sync
        def _(sp):
            sp.dma_start(xs[:, 0], tile_rows(x_rows, 0)).then_inc(S["x_in"], 16)
            sp.dma_start(cs[:, 0], tile_rows(ctx_rows, 0)).then_inc(cs_in[0], 16)
            sp.dma_start(xs[:, 1], tile_rows(x_rows, 1)).then_inc(S["x_in"], 16)
            for t in (2, 3):
                sp.dma_start(xs[:, t], tile_rows(x_rows, t)).then_inc(S["x_in_next"], 16)
            sp.dma_start(gates[:, 0:1], g_xattn.rearrange("(a b) -> a b", a=1).to_broadcast([P, 1])).then_inc(S["small_in"], 16)
            sp.dma_start(gates[:, 1:2], g_ffn.rearrange("(a b) -> a b", a=1).to_broadcast([P, 1])).then_inc(S["small_in"], 16)
            sp.dma_start(gates[:, 2:3], gamma.to_broadcast([P, 1])).then_inc(S["small_in"], 16)
            sp.dma_start(br[:], router_b.rearrange("(a e) -> a e", a=1).to_broadcast([P, E])).then_inc(S["small_in"], 16)
            sp.dma_start(wr_nat[:], router_w).then_inc(S["small_in"], 16)

            def stack_read(s, u, uh, r, b):
                sp.wait_ge(parts_out[r], 48 * (uh + 1))
                settle(sp)
                wait(sp, s, S["scores_T"], PAIRS * (u - 2) + HEADS * (b + 1))
                settle(sp)
                src = stacks[bass.ds(u, 1)].rearrange("o (two i) (d a) l -> (o i d) two a l", two=2, a=PAIRS)
                slot = 2 * r + b
                sp.dma_start(stk[0:STK, slot], src[:, :, HEADS * b:HEADS * (b + 1)]).then_inc(stk_in[slot], 16)

            def bias_load(to, rows, first, count):
                some = slice(first, first + count)
                sp.dma_start(to[:, some], rows[some].unsqueeze(0).to_broadcast([P, count, rows.shape[1]])).then_inc(S["bias_in"], 16)

            def slot_bias(slot, part):
                sp.wait_ge(S["scores_T"], HEADS * (2 * NT - 3 + slot))
                bias_load(bias_gu, gate_up_b, 4 * slot + 2 * part, 2)

            def sums_out(s, b):
                if s.on(1) if b else s.on(2):
                    n = 2 * s.tile(0)[0] + b - 3
                    sp.wait_ge(S["o_copied"], n + 1)
                    settle(sp)
                    sp.dma_start(att_raw[bass.ds(2 * n, 2)].rearrange("a p l -> p a l"),
                                 osb[:].rearrange("p (a l) -> p a l", a=2)).then_inc(o_out, 16)

            def body(s):
                t = None if s.loop else 2 * s.half + s.odd
                if s.on(3):
                    u, uh, r = s.tile(3)
                    sp.wait_ge(S["rden_ready"], u + 1)
                    settle(sp)
                    to = rden_dram[bass.ds(16 * u, 16)].rearrange("a (s i) -> (a s) i", s=8)
                    sp.dma_start(to, rden[:, r]).then_inc(S["rd_out"], 16)
                if s.on(0):
                    stack_read(s, *s.tile(0), 1)
                if t == 0:
                    for v in range(4, NT):
                        sp.dma_start(xs[:, v], tile_rows(x_rows, v)).then_inc(S["x_in_late"], 16)
                if s.on(-2) and (s.loop or t > -2):
                    u, uh, r = s.tile(-2)
                    wait(sp, s, S["rem_ready"], u - 1)
                    settle(sp)
                    sp.dma_start(cs[:, r], tile_rows(ctx_rows, u)).then_inc(cs_in[r], 16)
                if s.on(-1):
                    u, uh, r = s.tile(-1)
                    wait(sp, s, S["v_T"], u - 1)
                    settle(sp)
                    sp.dma_start(cv[:, r], ctx_rows[bass.ds(P * u, P)]).then_inc(cv_in[r], 16)
                if t == NT + 1:
                    slot_bias(1, 0)
                if s.on(1):
                    sp.wait_ge(S["m_T_copied"], 2 * s.tile(0)[0])
                    settle(sp)
                sums_out(s, 0)
                if s.on(3):
                    u, uh, r = s.tile(3)
                    sp.wait_ge(S["rd_out"], 16 * (u + 1))
                    settle(sp)
                    wait(sp, s, S["x1_ready"], u)
                    settle(sp)
                    src = rden_dram[bass.ds(16 * u, 16)].unsqueeze(0).to_broadcast([DH, 16, L])
                    sp.dma_start(rdb[:], src).then_inc(rdb_in, 16)
                if s.on(-1):
                    u, uh, r = s.tile(-1)
                    sp.wait_ge(S["split_ready"], u + 1)
                    settle(sp)
                    to = stacks[bass.ds(u, 1)].rearrange("o n p l -> p (o n) l")
                    for first, step, part, n in ((1, 2, Q3, 6), (2, 4, Q1, 3), (0, 4, Q2, 3)):
                        sp.dma_start(to[:, first:first + step * (n - 1) + 1:step],
                                     parts[:, r, part:part + n]).then_inc(parts_out[r], 16)
                if t == NT:
                    slot_bias(0, 0)
                if t == NT + 1:
                    slot_bias(1, 1)
                if s.on(2):
                    u, uh, r = s.tile(2)
                    sp.wait_ge(o_out, 32 * (u + 1))
                    settle(sp)
                    src = att_raw[bass.ds(4 * u, 4)].rearrange("a (j r) l -> r (a j) l", r=32)
                    wait(sp, s, S["rden_ready"], u - 1)
                    settle(sp)
                    sp.dma_start(den[:, r], src[DH].rearrange("a (s i) -> a s i", s=8)).then_inc(nat_in[r], 16)
                    wait(sp, s, S["x1_ready"], u - 1)
                    settle(sp)
                    sp.dma_start(nat[:, r], src[0:DH]).then_inc(nat_in[r], 16)
                if t == NT + 1:
                    slot_bias(2, 0)
                if t == NT + 2:
                    slot_bias(2, 1)
                    sp.wait_ge(sc_out[(NT - 3) % 2], 16 * TOPK * ((NT - 3) // 2 + 1))
                    settle(sp)
                    bias_load(bias_dn, down_b, 0, 4)
                    slot_bias(3, 0)
                    slot_bias(3, 1)
                if s.on(-1):
                    if t == -1:
                        sp.wait_ge(S["stacks_set"], 2)
                    stack_read(s, *s.tile(-1), 0)
                if t == NT:
                    slot_bias(0, 1)
                if s.on(0):
                    expert = s.tile(0)[0]
                    if s.loop or expert > 0:
                        sp.wait_ge(S["m_T_copied"], 2 * expert + 1)
                        settle(sp)
                    sp.dma_start(wgu[:, expert], gate_up[expert].rearrange("(c p) f -> p c f", p=P)).then_inc(S["w_in"], 16)
                    sp.dma_start(wdn[:, expert], down[expert].rearrange("(c p) f -> p c f", p=P)).then_inc(S["w_in"], 16)
                if t in range(4):
                    sp.wait_ge(S["zpay_set"], 1)
                    to = xd[4 * t * REGION:4 * (t + 1) * REGION].rearrange("(e r) f -> r e f", e=4)
                    sp.dma_start(to[0:P], zpay[:].unsqueeze(1).to_broadcast([P, 4, PW])).then_inc(S["zero_in"], 16)
                if t == 4:
                    sp.dma_start(xd[E * REGION:ROWS], zpay[:]).then_inc(S["zero_in"], 16)
                sums_out(s, 1)
                if t in (1, 2, 3):
                    bias_load(bias_dn, down_b, 4 * t, 4)

            steps(sp, body)

            sp.wait_ge(S["tile_rows_ready"], 1)
            sp.wait_ge(S["zero_in"], 16 * (E // 4 + 1))
            for r in range(2):
                sp.wait_ge(sc_out[r], 16 * TOPK * NT // 2)

            def expert_loads(quarter, r):
                i, iq, slot, on = etile(quarter, r, -1)
                if on:
                    if not isinstance(iq, int) or iq >= 1:
                        sp.wait_ge(S["x_T"], i - 3)
                        sp.wait_ge(S["dest_ready"], i - 3)
                    row = sp.value_load(tab_row[0:1, bass.ds(i, 1)], min_val=0, max_val=ROWS - P)
                    sp.dma_start(xt[:, slot], xd[bass.ds(row, P)]).then_inc(xt_in[slot], 16)
            chunk_loop(sp, expert_loads)

            for r in range(4):
                sp.wait_ge(y_out[r], 16 * ((MT + 3 - r) // 4))
            yv = yd.rearrange("(k t p) f -> t p k f", k=TOPK, p=P)
            for u in range(YSLOTS):
                sp.dma_start(yk[:, u], yv[u]).then_inc(yk_in[u], 16)
            for u in range(NT):
                sp.wait_ge(S["fin_ready"], u + 1)
                if u + YSLOTS < NT:
                    sp.dma_start(yk[:, u], yv[u + YSLOTS]).then_inc(yk_in[u], 16)
                sp.dma_start(tile_rows(out_rows, u), xs[:, u]).then_inc(fin_out, 16)
            sp.wait_ge(fin_out, 16 * NT)

        @block.gpsimd
        def _(pool):
            nc.gpsimd.memset(minus_half[:], -0.5).then_inc(S["half_set"], 1)
            pool.wait_ge(S["half_set"], 1)
            nc.gpsimd.memset(stk[:, :, 0].bitcast(F32), 0.0).then_inc(S["stacks_set"], 1)
            nc.gpsimd.memset(zpay[:, 0:H], 0.0)
            nc.gpsimd.memset(zpay[:, H:PW].bitcast(U32), SKIP).then_inc(S["zpay_set"], 1)

            def constants():
                link = chain(pool, S["setup_link"], 12, 0)
                link(nc.gpsimd.memset(ident[:], 0.0))
                link(nc.gpsimd.affine_select(out=ident[:], in_=ident[:], compare_op=ALU.not_equal, fill=1.0, base=0,
                                             pattern=[[-1, P]], channel_multiplier=1))
                link(nc.gpsimd.tensor_copy(identb[:], ident[:]))
                link(nc.gpsimd.memset(ones[:], 1.0))
                link(nc.gpsimd.affine_select(out=before[:], in_=ones[:], compare_op=ALU.is_gt, fill=0.0, base=0,
                                             pattern=[[1, P]], channel_multiplier=-1))
                nc.gpsimd.memset(vt[:, :, :, :, DH:2 * DH], 1.0)
                nc.gpsimd.memset(seen[:], 0.0)
                nc.gpsimd.iota(iota_i[:, 0], pattern=[[0, TOPK], [1, E]], base=0, channel_multiplier=0)
                nc.gpsimd.iota(iota_i[:, 1], pattern=[[TOK, TOPK], [0, E]], base=0, channel_multiplier=0)
                nc.gpsimd.iota(iota_i[:, 2], pattern=[[0, TOPK], [REGION, E]], base=P, channel_multiplier=0)
                link(nc.gpsimd.iota(tok_i[:], pattern=[[P, NT]], base=0, channel_multiplier=1))
                nc.gpsimd.tensor_copy(iota_f[:], iota_i[:])
                link(nc.gpsimd.tensor_copy(tok_f[:], tok_i[:]))
                nc.gpsimd.tensor_copy(tok_f[:], tok_f[:]).then_inc(S["consts"], 1)
                pool.wait_ge(S["consts"], 1)
                nc.gpsimd.memset(etab[:], 0.0)
                nc.gpsimd.memset(upto[:], 1.0)
                nc.gpsimd.tensor_scalar(minus_row[:], tok_f[:, 0:1], float(-P), float(-P), ALU.mult, ALU.add)
                nc.gpsimd.tensor_copy(tile_no[:], tok_f[:, 0:1]).then_inc(S["late_link"], 1)
                pool.wait_ge(S["late_link"], 1)
                nc.gpsimd.affine_select(out=upto[:], in_=upto[:], compare_op=ALU.is_ge, fill=0.0, base=0,
                                        pattern=[[1, E], [-1, E]], channel_multiplier=0).then_inc(S["late_consts"], 1)

            def rstd(rs, u, r, got, done):
                pool.wait_ge(got, u + 1)
                settle(pool)
                nc.gpsimd.tensor_tensor(rs[:, r, 1:2], rs[:, r, 0:1], minus_half[:], ALU.pow).then_inc(done, 1)

            def max_parts(s, b):
                n = 2 * s.tile(0)[0] + b
                b = b % 2
                pool.wait_ge(S["max_ready"], HEADS * (n + 1))
                link = chain(pool, S["mpart_link"], 3, n)
                wait(pool, s, S["m_T"], n - 1)
                settle(pool)
                link(nc.gpsimd.tensor_copy(mpart[:, b, 0], mx[:, b]))
                link(nc.gpsimd.tensor_tensor(mrem[:, b], mx[:, b], mpart[:, b, 0], ALU.subtract))
                settle(pool)
                link(nc.gpsimd.tensor_copy(mpart[:, b, 1], mrem[:, b]))
                nc.gpsimd.tensor_tensor(mpart[:, b, 2], mrem[:, b], mpart[:, b, 1], ALU.subtract).then_inc(S["mpart_ready"], 1)

            def scatter_rows(s, choices):
                u, uh, r = s.tile(5)
                pool.wait_ge(S["route2"], u + 1)
                settle(pool)
                for k in choices:
                    nc.gpsimd.indirect_dma_start(out=xd, out_offset=IndexOnAxis(slots[:, r, k:k + 1], 0),
                                                 in_=pay[:, r], in_offset=None).then_inc(sc_out[r], 16)

            def body(s):
                t = None if s.loop else 2 * s.half + s.odd
                tail = not s.loop and t > NT
                if t == -1:
                    constants()
                if s.on(1):
                    max_parts(s, -1)
                if s.on(4):
                    u, uh, r = s.tile(4)
                    rstd(rs2, u, r, S["var2"], S["rstd2"])
                if s.on(5):
                    scatter_rows(s, range(TOPK) if tail else (0,))
                if s.on(-2):
                    u, uh, r = s.tile(-2)
                    pool.wait_ge(S["k1_ready"], u + 1)
                    nc.gpsimd.tensor_tensor(kr[:], cs[:, r], parts[:, r, K1], ALU.subtract).then_inc(S["kr_ready"], 1)
                if s.on(5) and not tail:
                    scatter_rows(s, (1,))
                if s.on(-2):
                    u, uh, r = s.tile(-2)
                    rstd(rs1, u, r, S["var1"], S["rstd1"])
                if s.on(0):
                    max_parts(s, 0)
                if s.on(3):
                    u, uh, r = s.tile(3)
                    pool.wait_ge(nat_in[r], 32 * (uh + 1))
                    pool.wait_ge(rdb_in, 16 * (u + 1))
                    link = chain(pool, S["x1_link"], 1, u)
                    link(nc.gpsimd.tensor_tensor(nat[:, r], nat[:, r], rdb[:], ALU.mult))
                    nc.gpsimd.tensor_tensor(xs[:, u], xs[:, u], nat[:, r], ALU.add).then_inc(S["x1_ready"], 1)
                if s.on(-2):
                    u, uh, r = s.tile(-2)
                    pool.wait_ge(S["q1_ready"], u + 1)
                    nc.gpsimd.tensor_tensor(qf[:], qf[:], parts[:, r, Q1], ALU.subtract).then_inc(S["rem_ready"], 1)
                if s.on(-2):
                    u, uh, r = s.tile(-2)
                    pool.wait_ge(S["k2_ready"], u + 1)
                    nc.gpsimd.tensor_tensor(parts[:, r, K3], kr[:], parts[:, r, K2], ALU.subtract)
                    pool.wait_ge(S["q2_ready"], u + 1)
                    nc.gpsimd.tensor_tensor(parts[:, r, Q3], qf[:], parts[:, r, Q2], ALU.subtract).then_inc(S["split_ready"], 1)
                if s.on(5) and not tail:
                    scatter_rows(s, (2, 3))
            steps(pool, body)

            def scatter(quarter, r):
                i, iq, slot, on = etile(quarter, r, 2)
                if on:
                    pool.wait_ge(S["y_copied"], i + 1)
                    settle(pool)
                    nc.gpsimd.indirect_dma_start(out=yd, out_offset=IndexOnAxis(idxc[:, slot:slot + 1], 0),
                                                 in_=ysb[:, slot], in_offset=None, bounds_check=TOPK * TOK - 1,
                                                 oob_is_err=False).then_inc(y_out[slot], 16)
            chunk_loop(pool, scatter)

        @block.scalar
        def _(act_e):
            def body(s):
                if not s.loop and 2 * s.half + s.odd == -1:
                    act_e.wait_ge(S["small_in"], 80)
                    nc.scalar.activation(gates[:, 0:2], gates[:, 0:2], ACT.Tanh).then_inc(S["gates_ready"], 1)
                if not s.loop and 2 * s.half + s.odd == 0:
                    act_e.wait_ge(S["wr_T"], 1)
                    nc.scalar.copy(wr[:], HB[:, 0:HC * E].rearrange("p (c e) -> p c e", c=HC)).then_inc(S["wr_ready"], 1)
                for b in range(2):
                    for j in range(HEADS):
                        if s.on(1):
                            u = s.tile(1)[0]
                            n = PAIRS * u + HEADS * b + j
                            act_e.wait_ge(S["scores_T"], n + 1)
                            wait(act_e, s, S["pv_ready"], 2 * (2 * u + b - 1) + j // 4 + 1)
                            nc.scalar.activation(prob[:, j], ST[j % 2][:], ACT.Exp, scale=SCALE).then_inc(S["exp_ready"], 1)
                        at = HEADS * b + j
                        if s.on(-2):
                            u, uh, r = s.tile(-2)
                            if at == 5:
                                act_e.wait_ge(cs_in[r], 16 * (uh + 1))
                                wait(act_e, s, parts_out[r], 48 * uh)
                                wait(act_e, s, S["split_ready"], u)
                                nc.scalar.copy(parts[:, r, K1], cs[:, r]).then_inc(S["k1_ready"], 1)
                            if at == 10:
                                act_e.wait_ge(S["q_ready"], u + 1)
                                nc.scalar.copy(parts[:, r, Q1], qf[:]).then_inc(S["q1_ready"], 1)
                            if at == 9:
                                act_e.wait_ge(S["kr_ready"], u + 1)
                                nc.scalar.copy(parts[:, r, K2], kr[:]).then_inc(S["k2_ready"], 1)
                            if at == 13:
                                act_e.wait_ge(S["rem_ready"], u + 1)
                                nc.scalar.copy(parts[:, r, Q2], qf[:]).then_inc(S["q2_ready"], 1)
                        if at == 8 and s.on(0):
                            t, th, r = s.tile(0)
                            act_e.wait_ge(S["v_T"], t + 1)
                            wait(act_e, s, S["pv_ready"], 4 * (t - 1))
                            nc.scalar.copy(vt[:, r, :, :, 0:DH],
                                           HB[:, 0:2 * P].rearrange("p (c j v) -> p c j v", c=2, j=PAIRS)).then_inc(S["v_T_copied"], 1)
                        if j == 3 and (s.on(0) if b else s.on(1)):
                            n = 2 * s.tile(0)[0] + b - 1
                            rm = (b - 1) % 2
                            slot = (2 * s.odd + b - 1) % 4
                            act_e.wait_ge(S["m_T"], n + 1)
                            wait(act_e, s, mrow_in[(slot - 2) % 4], 16 * ((s.half if 2 * s.odd + b - 1 >= 0 else s.half - 1) + (1 if slot >= 2 else 0)))
                            nc.scalar.copy(mT[:, rm], MVB[0:MB_PARTS * PAIRS, 0:P // 2].bitcast(BF16)).then_inc(S["m_T_copied"], 1)
                        if j == 3 and (s.on(1) if b else s.on(2)):
                            n = 2 * s.tile(0)[0] + b - 3
                            act_e.wait_ge(S["pv_ready"], 2 * (n + 1))
                            wait(act_e, s, o_out, 16 * n)
                            nc.scalar.copy(osb[:], PV[:]).then_inc(S["o_copied"], 1)
                        if j == 4:
                            if s.on(0) if b else s.on(1):
                                n = 2 * s.tile(0)[0] + b - 1
                                slot = (2 * s.odd + b - 1) % 4
                                act_e.wait_ge(S["m_T_copied"], n + 1)
                                act_e.dma_start(stk[MROW:MROW + MB_PARTS, slot, 0], mT[:, (b - 1) % 2]).then_inc(mrow_in[slot], 16)
                        if at == 14 and s.on(2):
                            u, uh, r = s.tile(2)
                            act_e.wait_ge(S["pow_link"], u + 1)
                            nc.scalar.activation(rden[:, r], rden[:, r], ACT.Copy, scale=gates[:, 2:3]).then_inc(S["rden_ready"], 1)
                        if at == 7 and s.on(4):
                            u = s.tile(4)[0]
                            act_e.wait_ge(S["h_T"], u + 1)
                            wait(act_e, s, S["logits"], u)
                            nc.scalar.copy(hT[:], HB[:, 2 * P:4 * P].rearrange("p (c q) -> p c q", c=HC)).then_inc(S["h_T_copied"], 1)
            steps(act_e, body)

            act_e.wait_ge(S["wts_link"], 1)
            nc.scalar.activation(wts[:], wts[:], ACT.Exp).then_inc(S["exp_w"], 1)

            def expert_act(quarter, r):
                i, iq, slot, on = etile(quarter, r, -1)
                if on:
                    act_e.wait_ge(S["x_T"], i + 1)
                    if not isinstance(i, int) or i >= 2:
                        act_e.wait_ge(S["gu_ready"], i - 1)
                    nc.scalar.copy(xT[:, slot % 2], XTB[:, 0:H]).then_inc(S["x_T_copied"], 1)
                i, iq, slot, on = etile(quarter, r, 0)
                if on:
                    act_e.wait_ge(S["gate_ready"], i + 1)
                    if not isinstance(i, int) or i >= 2:
                        act_e.wait_ge(S["act_ready"], i - 1)
                    nc.scalar.activation(glu[:, slot % 2], gub[:, slot % 2, :, 0], ACT.Sigmoid, scale=ALPHA).then_inc(S["sig_ready"], 1)
                i, iq, slot, on = etile(quarter, r, 1)
                if on:
                    act_e.wait_ge(S["act_T"], i + 1)
                    if not isinstance(i, int) or i >= 2:
                        act_e.wait_ge(S["y_ready"], i - 1)
                    nc.scalar.copy(actT[:, slot % 2], ATB[:, 0:D]).then_inc(S["act_T_copied"], 1)
            chunk_loop(act_e, expert_act)

        @block.vector
        def _(dve):
            nc.vector.memset(PV[:], 0.0)
            def route(s, at):
                u, uh, r = s.tile(4)
                if s.on(4):
                    done = 9 * u
                    if at == 10:
                        dve.wait_ge(S["logits"], u + 1)
                        nc.vector.tensor_tensor(lg[:], RB[:, 0:E], br[:], ALU.add).then_inc(S["route_link"], 1)
                    if at == 11:
                        dve.wait_ge(S["route_link"], done + 1)
                        settle(dve)
                        nc.vector.max(best[:], lg[:]).then_inc(S["route_link"], 1)
                    if at == 12:
                        dve.wait_ge(S["route_link"], done + 2)
                        nc.vector.tensor_copy(top[:, bass.ds(u, 1)], best[:].unsqueeze(1))
                        nc.vector.max_index(tidx[:], best[:], lg[:]).then_inc(S["route_link"], 1)
                    if at == 13:
                        dve.wait_ge(S["route_link"], done + 3)
                        nc.vector.tensor_tensor(hot[:], e_iota, tidx[:, 0:TOPK].unsqueeze(2).to_broadcast([P, TOPK, E]),
                                                ALU.is_equal).then_inc(S["route_link"], 1)
                    if at == 14:
                        dve.wait_ge(S["route_link"], done + 4)
                        with nc.allow_low_precision("counts up to 16"):
                            nc.vector.tensor_reduce(pick[:, r], hot[:].rearrange("p k e -> p e k"), AX.X, ALU.add).then_inc(S["route_link"], 1)
                        nc.vector.tensor_tensor(tmp[:], hot[:], k_base, ALU.mult).then_inc(S["route_link"], 1)
                    if at == 15:
                        dve.wait_ge(S["route_link"], done + 6)
                        nc.vector.tensor_tensor(seen[:, 1 - r], seen[:, r], pick[:, r], ALU.add).then_inc(S["route1"], 1)
                        nc.vector.tensor_reduce(dst[:], tmp[:].rearrange("p k e -> p e k"), AX.X, ALU.add).then_inc(S["route_link"], 1)
                u, uh, r = s.tile(5)
                if s.on(5):
                    done = 9 * u + 7
                    if at == 0:
                        dve.wait_ge(S["route_link"], done)
                        settle(dve)
                        nc.vector.tensor_scalar(pay[:, r, H:PW].bitcast(U32), dst[:], tok_f[:, bass.ds(u, 1)], None, ALU.add)
                    if at == 1:
                        dve.wait_ge(S["ranks"], u + 1)
                        nc.vector.tensor_tensor(slot_base[:], RB[:, E:2 * E], e_region, ALU.add).then_inc(S["route_link"], 1)
                    if at == 2:
                        dve.wait_ge(S["route_link"], done + 1)
                        nc.vector.tensor_tensor(tmp[:], hot[:], slot_base[:].unsqueeze(1).to_broadcast([P, TOPK, E]),
                                                ALU.mult).then_inc(S["route_link"], 1)
                    if at == 3:
                        dve.wait_ge(S["route_link"], done + 2)
                        with nc.allow_low_precision("whole numbers under 2 ** 24"):
                            nc.vector.tensor_reduce(slots[:, r], tmp[:], AX.X, ALU.add).then_inc(S["route2"], 1)

            def body(s):
                if not s.loop and 2 * s.half + s.odd == -1:
                    nc.vector.memset(stk[:, :, 1].bitcast(U32), 0xBF80BF80).then_inc(S["stacks_set"], 1)
                if not s.loop and 2 * s.half + s.odd == 1:
                    dve.wait_ge(S["consts"], 1)
                    dve.wait_ge(S["gates_ready"], 1)
                    nc.vector.tensor_tensor(gates[:, 2:3], gates[:, 0:1], gates[:, 2:3], ALU.mult).then_inc(S["gates_ready"], 1)
                    dve.wait_ge(S["gates_ready"], 2)
                for at in range(PAIRS):
                    b, j = divmod(at, HEADS)
                    if s.on(0):
                        t = s.tile(0)[0]
                        dve.wait_ge(S["scores"], PAIRS * t + at + 1)
                        if j == 0:
                            wait(dve, s, S["mpart_ready"], 2 * t + b - 1)
                        nc.vector.tensor_reduce(mx[:, b, 2 * j:2 * j + 2], S1[j % 2][:].rearrange("p (c l) -> p c l", c=2),
                                                AX.X, ALU.max).then_inc(S["max_ready"], 1)
                    if s.on(4) and at == 0:
                        u, uh, r = s.tile(4)
                        dve.wait_ge(S["x1_ready"], u + 1)
                        nc.vector.bn_stats(st2[:], xs[:, u]).then_inc(S["stats2_link"], 1)
                    if s.on(4) and at == 1:
                        u, uh, r = s.tile(4)
                        dve.wait_ge(S["stats2_link"], u + 1)
                        settle(dve)
                        nc.vector.bn_aggr(mv2[:, r], st2[:]).then_inc(S["stats2"], 1)
                    if s.on(-2) and at == 5:
                        u, uh, r = s.tile(-2)
                        if s.loop or u >= 4:
                            dve.wait_ge(S["x_in_late"], 16 * (NT - 4))
                        elif u >= 2:
                            dve.wait_ge(S["x_in_next"], 32)
                        else:
                            dve.wait_ge(S["x_in"], 32)
                        nc.vector.bn_stats(st1[:], xs[:, u]).then_inc(S["stats1_link"], 1)
                    if s.on(-2) and at == 6:
                        u, uh, r = s.tile(-2)
                        dve.wait_ge(S["stats1_link"], u + 1)
                        settle(dve)
                        nc.vector.bn_aggr(mv1[:, r], st1[:]).then_inc(S["stats1"], 1)
                    if s.on(4) and at == 2:
                        u, uh, r = s.tile(4)
                        dve.wait_ge(S["stats2"], u + 1)
                        nc.vector.tensor_scalar(rs2[:, r, 0:1], mv2[:, r, 1:2], EPS, None, ALU.add).then_inc(S["var2"], 1)
                    if s.on(-2) and at == 7:
                        u, uh, r = s.tile(-2)
                        dve.wait_ge(S["stats1"], u + 1)
                        nc.vector.tensor_scalar(rs1[:, r, 0:1], mv1[:, r, 1:2], EPS, None, ALU.add).then_inc(S["var1"], 1)
                    if s.on(4) and at == 4:
                        u, uh, r = s.tile(4)
                        dve.wait_ge(S["rstd2"], u + 1)
                        wait(dve, s, sc_out[r], 16 * TOPK * uh)
                        nc.vector.tensor_scalar(pay[:, r, 0:H], xs[:, u], mv2[:, r, 0:1], rs2[:, r, 1:2],
                                                ALU.subtract, ALU.mult).then_inc(S["h_ready"], 1)
                    if s.on(-2) and at == 9:
                        u, uh, r = s.tile(-2)
                        dve.wait_ge(S["rstd1"], u + 1)
                        wait(dve, s, S["split_ready"], u)
                        nc.vector.tensor_scalar(qf[:], xs[:, u], mv1[:, r, 0:1], rs1[:, r, 1:2],
                                                ALU.subtract, ALU.mult).then_inc(S["q_ready"], 1)
                    if s.on(2) and at == 13:
                        u, uh, r = s.tile(2)
                        dve.wait_ge(nat_in[r], 32 * (uh + 1))
                        wait(dve, s, S["rd_out"], 16 * (u - 1))
                        nc.vector.reciprocal(rden[:, r], den[:, r]).then_inc(S["pow_link"], 1)
                    route(s, at)
            steps(dve, body)

            link = chain(dve, S["table_link"], 21, 0)
            dve.wait_ge(S["counts"], 1)
            dve.wait_ge(S["late_consts"], 1)
            link(nc.vector.tensor_copy(cnt[:], RB[:, 0:E]))
            link(nc.vector.tensor_scalar(cnti[:, 0], cnt[:], float(P - 1), None, ALU.add))
            link(nc.vector.tensor_scalar(cnti[:, 1], cnti[:, 0], 7, None, ALU.arith_shift_right))
            link(nc.vector.tensor_copy(tiles_of[:], cnti[:, 1]))
            link(nc.vector.tensor_tensor(sums[:], upto[:], tiles_of[:].unsqueeze(1).to_broadcast([P, E, E]), ALU.mult))
            link(nc.vector.tensor_reduce(ends[:], sums[:], AX.X, ALU.add))
            nc.vector.tensor_scalar(done[:], ends[:], tile_no[:], None, ALU.is_le)
            link(nc.vector.tensor_tensor(begins[:], ends[:], tiles_of[:], ALU.subtract))
            nc.vector.tensor_scalar(started[:], begins[:], tile_no[:], None, ALU.is_le)
            link(nc.vector.scalar_tensor_tensor(base[:], begins[:], float(P), cnt[:], ALU.mult, ALU.add))
            nc.vector.scalar_tensor_tensor(base[:], base[:], minus_row[:], e_region, ALU.add, ALU.add)
            link(nc.vector.tensor_tensor(held[:], started[:], done[:], ALU.subtract))
            nc.vector.tensor_reduce(ntab[:, 0:1], done[:], AX.X, ALU.add)
            link(nc.vector.tensor_tensor(held[:], held[:], base[:], ALU.mult))
            nc.vector.tensor_scalar(ntab[:, 1:2], ntab[:, 0:1], float(E), float(E * REGION), ALU.is_ge, ALU.mult)
            link(nc.vector.tensor_reduce(ntab[:, 2:3], held[:], AX.X, ALU.add))
            nc.vector.tensor_tensor(ntab[:, 2:3], ntab[:, 1:2], ntab[:, 2:3], ALU.add)
            nc.vector.tensor_scalar(ntab[:, 3:4], ntab[:, 0:1], float(E - 1), None, ALU.min).then_inc(S["tile_rows_T"], 1)
            dve.wait_ge(S["tile_rows_T"], 2)
            nc.vector.tensor_copy(tab_row[:], MVB[0:1, 0:MT]).then_inc(S["tile_rows_ready"], 1)
            link(nc.vector.tensor_copy(etab[:, 2:MT + 2], MVB[0:1, P:P + MT]))
            def tile_of_word(k):
                return etab[:, k:k + 4 * (MWORDS - 1) + 1:4]
            link(nc.vector.scalar_tensor_tensor(word[:], tile_of_word(5), 16.0, tile_of_word(4), ALU.mult, ALU.add))
            for k in (3, 2, 1):
                link(nc.vector.scalar_tensor_tensor(word[:], word[:], 16.0, tile_of_word(k), ALU.mult, ALU.add))
            nc.vector.scalar_tensor_tensor(tab_word[:], word[:], 16.0, tile_of_word(0), ALU.mult, ALU.add).then_inc(S["table_ready"], 1)
            wlink = chain(dve, S["wts_link"], 4, 0)
            wlink(nc.vector.tensor_tensor(wts[:], top[:, :, 0:TOPK], top[:, :, 0:1].to_broadcast([P, NT, TOPK]), ALU.subtract))
            dve.wait_ge(S["exp_w"], 1)
            wlink(nc.vector.tensor_reduce(wsum[:], wts[:], AX.X, ALU.add))
            wlink(nc.vector.reciprocal(wsum[:], wsum[:]))
            wlink(nc.vector.tensor_scalar(wsum[:], wsum[:], gates[:, 1:2], None, ALU.mult))
            nc.vector.tensor_tensor(wts[:], wts[:], wsum[:].unsqueeze(2).to_broadcast([P, NT, TOPK]), ALU.mult).then_inc(S["wts_ready"], 1)
            dve.wait_ge(S["table_ready"], 1)
            dve.wait_ge(S["bias_in"], 16 * 12)

            turn = {}

            def expert_dve(quarter, r):
                if r == 0:
                    turn["expert"] = experts_of(dve, quarter)
                i, iq, slot, on = etile(quarter, r, 0)
                gate, up = gub[:, slot % 2, :, 0], gub[:, slot % 2, :, 1]
                if on:
                    e = turn["expert"](r)
                    dve.wait_ge(xt_in[slot], 16 * (iq + 1))
                    if not isinstance(i, int) or i >= 4:
                        dve.wait_ge(y_out[slot], 16 * iq)
                    nc.vector.tensor_copy(idxc[:, slot:slot + 1], xt[:, slot, bass.ds(e + H, 1)].bitcast(U32)).then_inc(S["dest_ready"], 1)
                    dve.wait_ge(S["gu_ready"], i + 1)
                    link = chain(dve, S["act_link"], 2, i)
                    link(nc.vector.tensor_tensor(gub[:, slot % 2].rearrange("p f two -> p (f two)"), GU[slot % 2][:],
                                                 bias_gu[:, e], ALU.add))
                    nc.vector.tensor_scalar(gate, gate, LIMIT, None, ALU.min).then_inc(S["gate_ready"], 1)
                    nc.vector.tensor_scalar(up, up, LIMIT, -LIMIT, ALU.min, ALU.max)
                j, jq, jslot, jon = etile(quarter, r, 2)
                if jon:
                    ej = turn["expert"](r - 2)
                    dve.wait_ge(S["y_ready"], j + 1)
                    if not isinstance(j, int) or j >= 4:
                        dve.wait_ge(y_out[jslot], 16 * jq)
                    nc.vector.tensor_tensor(ysb[:, jslot], YB[jslot % 2][:, 0:H], bias_dn[:, ej], ALU.add).then_inc(S["y_copied"], 1)
                if on:
                    dve.wait_ge(S["sig_ready"], i + 1)
                    link(nc.vector.tensor_tensor(glu[:, slot % 2], gate, glu[:, slot % 2], ALU.mult))
                    if not isinstance(i, int) or i >= 2:
                        dve.wait_ge(S["act_T"], i - 1)
                    nc.vector.scalar_tensor_tensor(act[:, slot % 2], up, 1.0, glu[:, slot % 2], ALU.add, ALU.mult).then_inc(S["act_ready"], 1)
            chunk_loop(dve, expert_dve)

            for u in range(0, NT, 2):
                for k in range(TOPK):
                    for v in (u, u + 1):
                        if k == 0:
                            dve.wait_ge(yk_in[v % YSLOTS], 16 * (v // YSLOTS + 1))
                        else:
                            dve.wait_ge(S["sum_link"], 3 * u + 2 * (k - 1) + (v - u) + 1)
                        ins = nc.vector.scalar_tensor_tensor(xs[:, v], yk[:, v % YSLOTS, k], wts[:, v, k:k + 1],
                                                             xs[:, v], ALU.mult, ALU.add)
                        ins.then_inc(S["sum_link"] if k < TOPK - 1 else S["fin_ready"], 1)

        @block.tensor
        def _(pe):
            pe.wait_ge(S["consts"], 1)
            pe.wait_ge(S["small_in"], 80)
            for c in range(HC):
                ins = nc.tensor.transpose(HB[:, c * E:(c + 1) * E], wr_nat[:, c * P:(c + 1) * P], ident[0:E, 0:E])
            ins.then_inc(S["wr_T"], 1)
            pe.wait_ge(S["wr_ready"], 1)

            def value_product(s, n, lag, b, quad, c):
                u, uh, r = s.tile(lag)
                if c == 0:
                    pe.wait_ge(S["exp_ready"], HEADS * n + 4 * quad + 4)
                    if quad == 0:
                        wait(pe, s, S["o_copied"], n)
                        pe.wait_ge(S["v_T_copied"], u + 1)
                for jj in range(4):
                    j = 4 * quad + jj
                    ins = nc.tensor.matmul(PV[32 * jj:32 * jj + 2 * DH, quad * L:(quad + 1) * L],
                                           vt[:, r, c, HEADS * b + j], prob[:, j, c * L:(c + 1) * L],
                                           start=(c == 0), stop=(c == 1))
                if c == 1:
                    ins.then_inc(S["pv_ready"], 1)

            def body(s):
                t = s.tile(0)[0]
                for at in range(PAIRS):
                    b, j = divmod(at, HEADS)
                    if s.on(1):
                        u, uh, r = s.tile(1)
                        slot = 2 * r + b
                        n = PAIRS * u + at
                        if j == 0:
                            pe.wait_ge(mrow_in[slot], 16 * (uh + 1))
                        wait(pe, s, S["exp_ready"], n - 1)
                        for c in range(2):
                            ins = nc.tensor.matmul(ST[j % 2][:, c * L:(c + 1) * L],
                                                   stk[:, slot, 1, j, c * P:(c + 1) * P],
                                                   stk[:, slot, 0, j], start=True, stop=True)
                        ins.then_inc(S["scores_T"], 1)
                    if s.on(0):
                        t, th, r = s.tile(0)
                        slot = 2 * r + b
                        if j == 0:
                            pe.wait_ge(stk_in[slot], 16 * (th + 1))
                        wait(pe, s, S["max_ready"], PAIRS * t + at - 1)
                        for c in range(2):
                            ins = nc.tensor.matmul(S1[j % 2][:, c * L:(c + 1) * L],
                                                   stk[0:MROW, slot, 0, j, c * P:(c + 1) * P],
                                                   stk[0:MROW, slot, 1, j], start=True, stop=True)
                        ins.then_inc(S["scores"], 1)
                    if at == 0 and s.on(5):
                        u, uh, r = s.tile(5)
                        pe.wait_ge(S["route1"], u + 1)
                        nc.tensor.matmul(RB[:, E:2 * E], before[:], pick[:, r], start=True, stop=False)
                        nc.tensor.matmul(RB[:, E:2 * E], ones[:], seen[:, r], start=False, stop=True).then_inc(S["ranks"], 1)
                    if at == 4 and s.on(0):
                        t, th, r = s.tile(0)
                        pe.wait_ge(cv_in[r], 16 * (th + 1))
                        wait(pe, s, S["v_T_copied"], t)
                        for c in range(2):
                            ins = nc.tensor.transpose(HB[:, c * P:(c + 1) * P], cv[:, r, c * P:(c + 1) * P], ident[:])
                        ins.then_inc(S["v_T"], 1)
                    if j == 3 and (s.on(0) if b else s.on(1)):
                        n = 2 * t + b - 1
                        pe.wait_ge(S["mpart_ready"], n + 1)
                        wait(pe, s, S["m_T_copied"], n)
                        settle(pe)
                        nc.tensor.transpose(MVB[0:MB_PARTS * PAIRS, 0:P // 2].bitcast(BF16),
                                            mpart[:, (b - 1) % 2].rearrange("p s j -> p (s j)"),
                                            identb[:]).then_inc(S["m_T"], 1)
                    if at == 6 and s.on(4):
                        u, uh, r = s.tile(4)
                        pe.wait_ge(S["h_ready"], u + 1)
                        wait(pe, s, S["h_T_copied"], u)
                        for c in range(HC):
                            ins = nc.tensor.transpose(HB[:, (2 + c) * P:(3 + c) * P], pay[:, r, c * P:(c + 1) * P], ident[:])
                        ins.then_inc(S["h_T"], 1)
                    if at == 9 and s.on(4):
                        u = s.tile(4)[0]
                        pe.wait_ge(S["h_T_copied"], u + 1)
                        wait(pe, s, S["route1"], u)
                        for c in range(HC):
                            ins = nc.tensor.matmul(RB[:, 0:E], hT[:, c], wr[:, c], start=(c == 0), stop=(c == HC - 1))
                        ins.then_inc(S["logits"], 1)
                    if j in (1, 2):
                        lag = 1 if b else 2
                        if s.on(lag):
                            value_product(s, 2 * t + b - 3, lag, (b - 3) % 2, 1, j - 1)
                    if j in (5, 6) and s.on(1):
                        value_product(s, 2 * t + b - 2, 1, b, 0, j - 5)
            steps(pe, body)

            pe.wait_ge(S["route2"], NT)
            nc.tensor.matmul(RB[:, 0:E], ones[:], seen[:, NT % 2], start=True, stop=True).then_inc(S["counts"], 1)
            pe.wait_ge(S["tile_rows_T"], 1)
            nc.tensor.transpose(MVB[0:1, 0:MT], ntab[0:MT, 2:3], ident[0:MT, 0:MT])
            nc.tensor.transpose(MVB[0:1, P:P + MT], ntab[0:MT, 3:4], ident[0:MT, 0:MT]).then_inc(S["tile_rows_T"], 1)
            for _ in range(WARM):
                nc.tensor.matmul(ATB[:], ones[:], ones[:].unsqueeze(1).to_broadcast([P, 4, P]), start=True, stop=True)
            pe.wait_ge(S["table_ready"], 1)
            pe.wait_ge(S["w_in"], 32 * E)

            turn = {}

            def expert_pe(quarter, r):
                if r == 0:
                    turn["expert"] = experts_of(pe, quarter)
                i, iq, slot, on = etile(quarter, r, 0)
                if on:
                    e = turn["expert"](r)
                    pe.wait_ge(S["x_T_copied"], i + 1)
                    if not isinstance(i, int) or i >= 2:
                        pe.wait_ge(S["gate_ready"], i - 1)
                    for c in range(HC):
                        ins = nc.tensor.matmul(GU[slot % 2][:], xT[:, slot % 2, c * P:(c + 1) * P], wgu[:, e, c],
                                               start=(c == 0), stop=(c == HC - 1))
                    ins.then_inc(S["gu_ready"], 1)
                i, iq, slot, on = etile(quarter, r, -1)
                if on:
                    pe.wait_ge(xt_in[slot], 16 * (iq + 1))
                    if not isinstance(i, int) or i >= 1:
                        pe.wait_ge(S["x_T_copied"], i)
                    for c in range(HC):
                        ins = nc.tensor.transpose(XTB[:, c * P:(c + 1) * P], xt[:, slot, c * P:(c + 1) * P], ident[:])
                    ins.then_inc(S["x_T"], 1)
                i, iq, slot, on = etile(quarter, r, 2)
                if on:
                    e = turn["expert"](r - 2)
                    pe.wait_ge(S["act_T_copied"], i + 1)
                    if not isinstance(i, int) or i >= 2:
                        pe.wait_ge(S["y_copied"], i - 1)
                    for c in range(HC):
                        ins = nc.tensor.matmul(YB[slot % 2][:, 0:H], actT[:, slot % 2, c * P:(c + 1) * P], wdn[:, e, c],
                                               start=(c == 0), stop=(c == HC - 1))
                    ins.then_inc(S["y_ready"], 1)
                i, iq, slot, on = etile(quarter, r, 1)
                if on:
                    pe.wait_ge(S["act_ready"], i + 1)
                    if not isinstance(i, int) or i >= 1:
                        pe.wait_ge(S["act_T_copied"], i)
                    for c in range(HC):
                        ins = nc.tensor.transpose(ATB[:, c * P:(c + 1) * P], act[:, slot % 2, c * P:(c + 1) * P], ident[:])
                    ins.then_inc(S["act_T"], 1)
            chunk_loop(pe, expert_pe)


_INS = ["x", "ctx_2048", "g_xattn", "g_ffn", "L0_xattn_gamma", "L0_ffn_router_weight", "L0_ffn_router_bias",
        "L0_ffn_gate_up_proj", "L0_ffn_gate_up_proj_bias", "L0_ffn_down_proj", "L0_ffn_down_proj_bias"]


def kernel(**inputs):
    import numpy as np
    import concourse.bacc as bacc
    from concourse.bass_utils import run_bass_kernel_spmd

    nc = bacc.Bacc("TRN2", target_bir_lowering=False, num_devices=1)
    arrays, args = {}, []
    for name in _INS:
        a = np.ascontiguousarray(inputs[name])
        if a.ndim == 0:
            a = a.reshape(1, 1)
        arrays[f"in_{name}"] = a
        args.append(nc.dram_tensor(f"in_{name}", a.shape, mybir.dt.from_np(a.dtype), kind="ExternalInput").ap())
    out = nc.dram_tensor("out_x", inputs["x"].shape, F32, kind="ExternalOutput").ap()
    flamingo_gated_kernel(nc, *args, out)
    r = run_bass_kernel_spmd(nc, [arrays], core_ids=[0])
    return r.results[0]["out_x"]
```
